# Optimizing a Trainium2 kernel written in Bass

```python
import numpy as np
import jax
import jax.numpy as jnp

def _softmax(x, axis=-1):
    return jax.nn.softmax(x, axis=axis)

def _gelu(x):
    return jax.nn.gelu(x, approximate=True)

def _silu(x):
    return jax.nn.silu(x)

def _sigmoid(x):
    return jax.nn.sigmoid(x)

def _layernorm(x, axis=-1, eps=1e-05):
    m = jnp.mean(x, axis=axis, keepdims=True)
    v = jnp.var(x, axis=axis, keepdims=True)
    return (x - m) / jnp.sqrt(v + eps)

def _scatter_add(tgt, idx, src, axis=0):
    return tgt.at[idx].add(src)

def _segment_sum(src, seg, n):
    return jax.ops.segment_sum(src, seg, n)
kernel_name = 'mk_adj_ffn_d1_adj_r2_f8a32e'

def setup_inputs(seed: int=0):
    np.random.seed(seed)
    _w = jnp.asarray

    def _rec_inputs():
        import jax
        import jax.numpy as jnp
        _gk = jax.random.key(seed)
        x = -0.0005207 + 1.001 * jax.random.normal(jax.random.fold_in(_gk, 1), (2048, 128), jnp.float32)
        _a = jax.random.bernoulli(jax.random.fold_in(_gk, 2), 0.00390625, (2048, 2048))
        _a = jnp.logical_or(_a, jnp.swapaxes(_a, -1, -2))
        _a = jnp.logical_or(_a, jnp.eye(2048, dtype=bool))
        _af = _a.astype(jnp.float32)
        _af = _af * jax.random.uniform(jax.random.fold_in(_gk, 3), (2048, 2048), jnp.float32, 0.05, 1)
        adj = _af
        return (x, adj)
    x, adj = _rec_inputs()

    def _L0_gnn_setup():
        import jax, jax.numpy as jnp
        import numpy as np
        key = jax.random.key(seed)
        k1, k2, k3, k4 = jax.random.split(key, 4)
        N, F_in, F_out = (4096, 128, 128)
        x = jax.random.normal(k1, (N, F_in), dtype=jnp.float32)
        adj = jax.random.uniform(k2, (N, N), dtype=jnp.float32)
        lim = 1.0 / np.sqrt(F_in)
        W = jax.random.uniform(k3, (F_out, F_in), dtype=jnp.float32, minval=-lim, maxval=lim)
        b = jax.random.uniform(k4, (F_out,), dtype=jnp.float32, minval=-lim, maxval=lim)
        return {'x': x, 'adj': adj, 'W': W, 'b': b}
    _L0_gnn_all = _L0_gnn_setup()
    _L0_gnn_in = {k: v for k, v in _L0_gnn_all.items() if k in ('W', 'b')}
    del _L0_gnn_all

    def _L0_ffn_setup():
        import jax, jax.numpy as jnp
        import numpy as np
        D_MODEL = 128
        N_EXPERTS = 16
        HIDDEN = 256
        SCALE = 0.02
        key = jax.random.key(seed)
        ks = jax.random.split(key, 5)
        x = jax.random.normal(ks[0], (4, 4096, D_MODEL), dtype=jnp.float32)
        gate_w = jax.random.normal(ks[1], (D_MODEL, N_EXPERTS), dtype=jnp.float32) * SCALE
        gate_b = jnp.zeros((N_EXPERTS,), dtype=jnp.float32)
        w1 = jax.random.normal(ks[2], (N_EXPERTS, D_MODEL, HIDDEN), dtype=jnp.float32) * SCALE
        w2 = jax.random.normal(ks[3], (N_EXPERTS, D_MODEL, HIDDEN), dtype=jnp.float32) * SCALE
        w3 = jax.random.normal(ks[4], (N_EXPERTS, HIDDEN, D_MODEL), dtype=jnp.float32) * SCALE
        return {'x': x, 'gate_w': gate_w, 'gate_b': gate_b, 'w1': w1, 'w2': w2, 'w3': w3}
    _L0_ffn_all = _L0_ffn_setup()
    _L0_ffn_in = {k: v for k, v in _L0_ffn_all.items() if k in ('gate_w', 'gate_b', 'w1', 'w2', 'w3')}
    del _L0_ffn_all
    return {'x': x, 'adj': adj, 'L0_gnn_W': _L0_gnn_in['W'], 'L0_gnn_b': _L0_gnn_in['b'], 'L0_ffn_gate_w': _L0_ffn_in['gate_w'], 'L0_ffn_gate_b': _L0_ffn_in['gate_b'], 'L0_ffn_w1': _L0_ffn_in['w1'], 'L0_ffn_w2': _L0_ffn_in['w2'], 'L0_ffn_w3': _L0_ffn_in['w3']}

def reference(x, adj, L0_gnn_W, L0_gnn_b, L0_ffn_gate_w, L0_ffn_gate_b, L0_ffn_w1, L0_ffn_w2, L0_ffn_w3):
    import jax
    import jax.numpy as jnp

    def _L0_gnn_ref(x, adj, W, b):
        import jax, jax.numpy as jnp
        import numpy as np
        N = adj.shape[0]
        adj = adj + jnp.eye(N, dtype=adj.dtype)
        deg = adj.sum(axis=1)
        deg_inv_sqrt = deg ** (-0.5)
        deg_inv_sqrt = jnp.where(jnp.isinf(deg_inv_sqrt), 0.0, deg_inv_sqrt)
        adj_normalized = deg_inv_sqrt[:, None] * adj * deg_inv_sqrt[None, :]
        support = x @ W.T + b
        return adj_normalized @ support

    def _L0_ffn_ref(x, gate_w, gate_b, w1, w2, w3):
        import jax, jax.numpy as jnp
        import numpy as np
        D_MODEL = 128
        N_EXPERTS = 16
        HIDDEN = 256
        SCALE = 0.02
        n_experts = w1.shape[0]
        logits = jnp.einsum('bsd,de->bse', x, gate_w) + gate_b
        probs = jax.nn.softmax(logits, axis=-1)
        top_probs, top_idx = jax.lax.top_k(probs, 2)
        top_probs = top_probs / jnp.sum(top_probs, axis=-1, keepdims=True)
        dispatch = jnp.sum(jax.nn.one_hot(top_idx, n_experts, dtype=x.dtype) * top_probs[..., None], axis=-2)
        h1 = jnp.einsum('bsd,edh->bseh', x, w1)
        h2 = jnp.einsum('bsd,edh->bseh', x, w2)
        hidden = jax.nn.silu(h1) * h2
        expert_out = jnp.einsum('bseh,eho->bseo', hidden, w3)
        return jnp.einsum('bseo,bse->bso', expert_out, dispatch)
    x = x + _L0_gnn_ref(_layernorm(x, axis=-1), adj, L0_gnn_W, L0_gnn_b)
    x = x + _L0_ffn_ref(_layernorm(x, axis=-1)[None], L0_ffn_gate_w, L0_ffn_gate_b, L0_ffn_w1, L0_ffn_w2, L0_ffn_w3)[0]
    return x

_drawn_inputs = setup_inputs


def setup_inputs(seed=0):
    import zlib

    import numpy as np

    out = dict(_drawn_inputs(seed))
    spreads = {'L0_ffn_gate_b': (0.0, 0.8)}
    factors = {'L0_ffn_gate_w': 8.0, 'L0_ffn_w1': 8.0, 'L0_ffn_w2': 8.0, 'L0_ffn_w3': 8.0}
    for name, (base, spread) in spreads.items():
        noise = np.random.default_rng([zlib.crc32(name.encode()), seed]).standard_normal(out[name].shape)
        drawn = base * np.exp(spread * noise) if base else spread * noise
        out[name] = jnp.asarray(drawn.astype(out[name].dtype))
    for name, factor in factors.items():
        out[name] = (out[name] * factor).astype(out[name].dtype)
    return out
```

```python
from contextlib import ExitStack

import numpy as np

import concourse.bass as bass
from concourse import mybir

F32 = mybir.dt.float32
BF16 = mybir.dt.bfloat16
I32 = mybir.dt.int32
U32 = mybir.dt.uint32
ALU = mybir.AluOpType
ACT = mybir.ActivationFunctionType
AX_X = mybir.AxisListType.X

P = 128
BANK = 512
EPS = 1e-5


def graph_moe(nc, x, adj, w_gnn, b_gnn, gate_w, gate_b, w1, w2, w3, out):
    N, D = x.shape
    E, _, HID = w1.shape
    NT = N // P
    TOPK = 2
    RING = 4
    EAGER = BANK // P
    NPAIR = NT // 2
    BLOCKS = BANK // P
    GROUPS = NT // BLOCKS
    HALF = N // 2
    HC = HID // P
    REGION = P + N
    NULL_ROW = E * REGION
    SLOTS = TOPK * N
    NTILE = SLOTS // P + E - 1
    ROW = D + 2
    NTP = NTILE + 1
    assert D == P and HC == 2 and 2 * HID == BANK and NT % RING == 0 and EAGER == RING

    with ExitStack() as ctx:
        def sb(name, shape, dtype=F32):
            return ctx.enter_context(nc.sbuf_tensor(name, shape, dtype))

        def sem(name):
            return ctx.enter_context(nc.semaphore(name))

        x_sorted = nc.dram_tensor("x_sorted", [NULL_ROW + P, ROW], F32, kind="Internal").ap()
        y_tokens = nc.dram_tensor("y_tokens", [SLOTS, D], F32, kind="Internal").ap()

        adjT = sb("adjT", [P, NT * N])
        a_rows = sb("a_rows", [P, RING, N])
        folded = sb("folded", [P, 2, HALF])
        x_mid = sb("x_mid", [P, NT, D])
        support = sb("support", [P, NT, D])
        scaled = sb("scaled", [P, NT, D])
        scaled_now = sb("scaled_now", [P, RING, D])
        w_nat = sb("w_nat", [P, D])
        w_t = sb("w_t", [P, D])
        b_row = sb("b_row", [1, D])
        gate_sb = sb("gate_sb", [P, E])
        gate_b_row = sb("gate_b_row", [1, E])
        ident = sb("ident", [P, P])
        ones_row = sb("ones_row", [1, P])
        before = sb("before", [P, P], BF16)
        ones = sb("ones", [P, P], BF16)
        iota_e = sb("iota_e", [P, E])
        region_row = sb("region_row", [1, E])
        region_col = sb("region_col", [NTP, E])
        tile_no = sb("tile_no", [NTP, 1])
        tile_row = sb("tile_row", [NTP, 1])
        dest = sb("dest", [P, NT, TOPK], I32)
        minus_half = sb("minus_half", [P, NT])
        pad = sb("pad", [P, ROW])
        xn_t = sb("xn_t", [P, 2, D])
        x_stats = sb("x_stats", [P, NT, 6])
        x_mv = sb("x_mv", [P, NT, 2])
        x_var = sb("x_var", [P, NT])
        x_rstd = sb("x_rstd", [P, NT])
        row_sum = sb("row_sum", [P, NT])
        no_degree = sb("no_degree", [P, NT])
        degree = sb("degree", [P, NT])
        root = sb("root", [P, NT])
        dinv = sb("dinv", [P, NT])
        stats = sb("stats", [P, 2, 6])
        mv = sb("mv", [P, 2, 2])
        var = sb("var", [P, 2])
        rstd = sb("rstd", [P, 2])
        best = sb("best", [P, 2, 8])
        best_at = sb("best_at", [P, 2, 8], U32)
        gap = sb("gap", [P, 2])
        e_gap = sb("e_gap", [P, 2])
        e_sum = sb("e_sum", [P, 2])
        chosen = sb("chosen", [P, TOPK, 2, E])
        member = sb("member", [P, 2, 2, E], BF16)
        members = sb("members", [P, 3, E], BF16)
        picked = sb("picked", [P, TOPK, 2, E])
        slot_f = sb("slot_f", [P, TOPK, 2])
        slot = sb("slot", [P, 2, TOPK, 2], U32)
        cnt = sb("cnt", [NTP, E])
        cnt_up = sb("cnt_up", [NTP, E], I32)
        tiles_i = sb("tiles_i", [NTP, E], I32)
        tiles_f = sb("tiles_f", [NTP, E])
        zeros_e = sb("zeros_e", [NTP, E])
        upto = sb("upto", [NTP, E])
        prior = sb("prior", [NTP, E])
        end_row = sb("end_row", [NTP, E])
        passed = sb("passed", [NTP, E])
        is_own = sb("is_own", [NTP, E])
        n_passed = sb("n_passed", [NTP, 1])
        live = sb("live", [NTP, 1])
        start_sum = sb("start_sum", [NTP, 1])
        table_col = sb("table_col", [NTP, 2])
        table = sb("table", [1, 2 * NTP], I32)
        meta = sb("meta", [P, RING, 2])
        y_dest = sb("y_dest", [P, RING, 1])

        w12_at, w3_at, z_at = 0, EAGER * N, 8 * N
        w12 = adjT[:, w12_at:w12_at + E * BANK]
        w3s = adjT[:, w3_at:w3_at + E * HID]
        z_buf = adjT[:, z_at:z_at + NT * TOPK * D].rearrange("p (i k d) -> p i k d", k=TOPK, d=D)

        late = a_rows[:].rearrange("p u n -> p (u n)")
        used = 0

        def over(shape, pattern=None, **sizes):
            nonlocal used
            n = int(np.prod(shape))
            part = late[:, used:used + n]
            used += n
            return part.rearrange(pattern, **sizes) if pattern else part

        acc_sb = over([2, 2, P], "p (c t n) -> p c t n", c=2, t=2)
        rows = over([2, 2, TOPK, ROW], "p (c t k n) -> p c t k n", c=2, t=2, k=TOPK)
        xT2 = over([2, 2, P], "p (c t n) -> p c t n", c=2, t=2)
        xg = over([RING, ROW], "p (u n) -> p u n", u=RING)
        xgT = over([2, P], "p (u n) -> p u n", u=2)
        sil = over([2, HID], "p (u n) -> p u n", u=2)
        hid = over([2, HID], "p (u n) -> p u n", u=2)
        hidT = over([2, HID], "p (u n) -> p u n", u=2)
        y_out = over([RING, D], "p (u n) -> p u n", u=RING)
        assert used <= RING * N

        bank = [ctx.enter_context(nc.psum_tensor(f"bank{i}", [P, BANK], F32)) for i in range(8)]

        consts = sem("consts")
        fill = sem("fill")
        x_loaded = sem("x_loaded")
        par_loaded = sem("par_loaded")
        a_loaded = [sem(f"a_loaded{i}") for i in range(RING)]
        x_stat = sem("x_stat")
        x_var_ready = sem("x_var_ready")
        x_rstd_ready = sem("x_rstd_ready")
        xn_ready = sem("xn_ready")
        wt_psum = sem("wt_psum")
        wt_ready = sem("wt_ready")
        xnt_psum = sem("xnt_psum")
        xnt_ready = sem("xnt_ready")
        sup_psum = sem("sup_psum")
        sup_ready = sem("sup_ready")
        transposed = sem("transposed")
        copied = sem("copied")
        fold_done = sem("fold_done")
        row_step = sem("row_step")
        root_ready = sem("root_ready")
        scale_step = sem("scale_step")
        eager_done = sem("eager_done")
        acc_done = sem("acc_done")
        acc_copied = sem("acc_copied")
        back_psum = sem("back_psum")
        mix_step = sem("mix_step")
        var_ready = sem("var_ready")
        rstd_ready = sem("rstd_ready")
        rows_ready = sem("rows_ready")
        dest_ready = sem("dest_ready")
        rowsT_psum = sem("rowsT_psum")
        rowsT_ready = sem("rowsT_ready")
        logits_psum = sem("logits_psum")
        gap_ready = sem("gap_ready")
        e_ready = sem("e_ready")
        pick_step = sem("pick_step")
        member_ready = sem("member_ready")
        members_ready = sem("members_ready")
        rank_psum = sem("rank_psum")
        gate_step = sem("gate_step")
        slot_ready = sem("slot_ready")
        rows_sent = [sem(f"rows_sent{i}") for i in range(2)]
        pads_sent = sem("pads_sent")
        count_psum = sem("count_psum")
        tab_step = sem("tab_step")
        tab_psum = sem("tab_psum")
        table_ready = sem("table_ready")
        w_loaded = sem("w_loaded")
        xg_loaded = [sem(f"xg_loaded{i}") for i in range(RING)]
        xgT_psum = sem("xgT_psum")
        xgT_ready = sem("xgT_ready")
        meta_ready = sem("meta_ready")
        h_psum = sem("h_psum")
        sil_ready = sem("sil_ready")
        hid_ready = sem("hid_ready")
        hidT_psum = sem("hidT_psum")
        hidT_ready = sem("hidT_ready")
        y_psum = sem("y_psum")
        y_ready = sem("y_ready")
        y_sent = [sem(f"y_sent{i}") for i in range(RING)]
        z_loaded = [sem(f"z_loaded{i}") for i in range(RING)]
        z_sum = sem("z_sum")
        out_ready = sem("out_ready")
        out_sent = sem("out_sent")

        NCONST = 14

        LAG = 3
        FULL = NTILE - LAG
        assert FULL % RING == 0

        def steps(eng, step):
            head = LAG + RING
            for s in range(head):
                step(s, s % RING, s // RING, range(min(s, LAG) + 1))
            with eng.Fori(0, FULL // RING - 1) as r:
                for s in range(head, head + RING):
                    step(RING * r + s, s % RING, r + s // RING, range(LAG + 1))
            for s in range(NTILE, NTILE + LAG):
                step(s, s % RING, s // RING, range(s - NTILE + 1, LAG + 1))

        block = ctx.enter_context(nc.Block())

        @block.sync
        def _(sp):
            sp.dma_start(x_mid[:], x.rearrange("(i p) d -> p i d", p=P)).then_inc(x_loaded, 16)
            sp.dma_start(w_nat[:], w_gnn).then_inc(par_loaded, 16)
            sp.dma_start(b_row[:], b_gnn.rearrange("(a n) -> a n", a=1)).then_inc(par_loaded, 16)
            sp.dma_start(gate_sb[:], gate_w).then_inc(par_loaded, 16)
            sp.dma_start(gate_b_row[:], gate_b.rearrange("(a n) -> a n", a=1)).then_inc(par_loaded, 16)

            def load_rows(k, u):
                sp.dma_start(a_rows[:, u, :], adj[bass.ds(k * P, P), :]).then_inc(a_loaded[u], 16)

            for u in range(RING):
                load_rows(u, u)
            with sp.Fori(0, NT // RING - 1) as r:
                for u in range(RING):
                    sp.wait_ge(transposed, (RING * r + u + 1) * GROUPS)
                    sp.wait_ge(fold_done, RING * r + u + 1)
                    load_rows(RING * r + u + RING, u)
            sp.wait_ge(consts, NCONST)
            for e in range(E + 1):
                sp.dma_start(x_sorted[e * REGION:e * REGION + P, :], pad[:]).then_inc(pads_sent, 16)
            sp.wait_ge(eager_done, 1)
            w12_v = w12.rearrange("p (e n) -> p e n", e=E)
            sp.dma_start(w12_v[:, :, 0:HID], w1.rearrange("e d h -> d e h")).then_inc(w_loaded, 16)
            sp.dma_start(w12_v[:, :, HID:BANK], w2.rearrange("e d h -> d e h")).then_inc(w_loaded, 16)
            sp.wait_ge(acc_done, 1)
            for c in range(HC):
                sp.dma_start(w3s.rearrange("p (e c d) -> p e c d", e=E, c=HC)[:, :, c, :],
                             w3[:, c * P:(c + 1) * P, :].rearrange("e h d -> h e d")).then_inc(w_loaded, 16)

            for i in range(2):
                sp.wait_ge(rows_sent[i], 16 * 2 * TOPK * NPAIR // 2)
            sp.wait_ge(pads_sent, 16 * (E + 1))
            sp.wait_ge(table_ready, 1)

            def load_tile(t, u):
                first = sp.value_load(table[0:1, bass.ds(t, 1)], min_val=0, max_val=NULL_ROW)
                sp.dma_start(xg[:, u, :], x_sorted[bass.ds(first, P), :]).then_inc(xg_loaded[u], 16)

            for t in range(RING):
                load_tile(t, t)
            rounds = NTILE // RING
            with sp.Fori(0, rounds - 1) as r:
                for u in range(RING):
                    sp.wait_ge(meta_ready, RING * r + u + 1)
                    load_tile(RING * r + u + RING, u)
            for t in range(RING * rounds, NTILE):
                sp.wait_ge(meta_ready, t - RING + 1)
                load_tile(t, t % RING)

            for u in range(RING):
                sp.wait_ge(y_sent[u], 16 * len(range(u, NTILE, RING)))
            z_dram = y_tokens.rearrange("(i p k) d -> p i (k d)", p=P, k=TOPK)
            for q in range(RING):
                part = slice(q * NT // RING, (q + 1) * NT // RING)
                sp.dma_start(z_buf[:, part].rearrange("p i k d -> p i (k d)"), z_dram[:, part]).then_inc(z_loaded[q], 16)
            out_v = out.rearrange("(i p) d -> p i d", p=P)
            for q in range(RING):
                part = slice(q * NT // RING, (q + 1) * NT // RING)
                sp.wait_ge(out_ready, q + 1)
                sp.dma_start(out_v[:, part], x_mid[:, part]).then_inc(out_sent, 16)
            sp.wait_ge(out_sent, 16 * RING)

        @block.gpsimd
        def _(pool):
            nc.gpsimd.memset(ident[:], 0.0).then_inc(fill, 1)
            nc.gpsimd.memset(before[:], 1.0).then_inc(fill, 1)
            nc.gpsimd.memset(pad[:], 0.0).then_inc(fill, 1)
            pool.wait_ge(fill, 3)
            nc.gpsimd.affine_select(out=ident[:], in_=ident[:], compare_op=ALU.not_equal, fill=1.0, base=0,
                                    pattern=[[-1, P]], channel_multiplier=1).then_inc(consts, 1)
            nc.gpsimd.memset(minus_half[:], -0.5).then_inc(consts, 1)
            nc.gpsimd.memset(ones_row[:], 1.0).then_inc(consts, 1)
            nc.gpsimd.affine_select(out=before[:], in_=before[:], compare_op=ALU.is_gt, fill=0.0, base=0,
                                    pattern=[[1, P]], channel_multiplier=-1).then_inc(consts, 1)
            nc.gpsimd.memset(ones[:], 1.0).then_inc(consts, 1)
            nc.gpsimd.memset(members[:], 0.0).then_inc(consts, 1)
            nc.gpsimd.memset(zeros_e[:], 0.0).then_inc(consts, 1)
            exact = dict(allow_small_or_imprecise_dtypes=True)
            nc.gpsimd.iota(iota_e[:], pattern=[[1, E]], base=0, channel_multiplier=0, **exact).then_inc(consts, 1)
            nc.gpsimd.iota(region_row[:], pattern=[[REGION, E]], base=P, channel_multiplier=0, **exact).then_inc(consts, 1)
            nc.gpsimd.iota(region_col[:], pattern=[[REGION, E]], base=0, channel_multiplier=0, **exact).then_inc(consts, 1)
            nc.gpsimd.iota(tile_no[:], pattern=[[0, 1]], base=0, channel_multiplier=1, **exact).then_inc(consts, 1)
            nc.gpsimd.iota(tile_row[:], pattern=[[0, 1]], base=0, channel_multiplier=P, **exact).then_inc(consts, 1)
            nc.gpsimd.iota(dest[:], pattern=[[TOPK * P, NT], [1, TOPK]], base=0, channel_multiplier=TOPK).then_inc(consts, 1)
            nc.gpsimd.iota(pad[:, D + 1:ROW].bitcast(I32), pattern=[[0, 1]], base=SLOTS, channel_multiplier=0).then_inc(consts, 1)

            pool.wait_ge(consts, 2)
            pool.wait_ge(x_var_ready, 1)
            nc.gpsimd.tensor_tensor(x_rstd[:], x_var[:], minus_half[:], ALU.pow).then_inc(x_rstd_ready, 1)

            def fold(k, u, q, first=False):
                pool.wait_ge(a_loaded[u], 16 * (q + 1))
                if not first:
                    pool.wait_ge(row_step, 3 * (k - 1) - 2)
                nc.gpsimd.tensor_tensor(folded[:, u % 2, :], a_rows[:, u, 0:HALF], a_rows[:, u, HALF:N],
                                        ALU.add).then_inc(fold_done, 1)

            def take_root(k):
                pool.wait_ge(row_step, 3 * k + 3)
                nc.gpsimd.tensor_tensor(root[:, bass.ds(k, 1)], degree[:, bass.ds(k, 1)],
                                        minus_half[:, 0:1], ALU.pow).then_inc(root_ready, 1)

            for k in range(RING):
                fold(k, k, 0, first=k < 2)
                if k:
                    take_root(k - 1)
            with pool.Fori(0, NT // RING - 1) as r:
                for u in range(RING):
                    fold(RING * r + (RING + u), u, r + 1)
                    take_root(RING * r + (RING + u - 1))
            take_root(NT - 1)

            def pair_root(c):
                pool.wait_ge(var_ready, c + 1)
                nc.gpsimd.tensor_tensor(rstd[:], var[:], minus_half[:, 0:2], ALU.pow).then_inc(rstd_ready, 1)

            def send_rows(c, u):
                pool.wait_ge(slot_ready, c + 1)
                pool.wait_ge(dest_ready, c + 1)
                for t in range(2):
                    for k in range(TOPK):
                        nc.gpsimd.indirect_dma_start(
                            x_sorted, bass.IndirectOffsetOnAxis(ap=slot[:, u, k, t:t + 1], axis=0),
                            rows[:, u, t, k, :], None).then_inc(rows_sent[u], 16)

            pair_root(0)
            for c in range(NPAIR):
                if c + 1 < NPAIR:
                    pair_root(c + 1)
                send_rows(c, c % 2)

            for t in range(NTILE):
                u = t % RING
                pool.wait_ge(y_ready, t + 1)
                nc.gpsimd.indirect_dma_start(
                    y_tokens, bass.IndirectOffsetOnAxis(ap=y_dest[:, u, :].bitcast(U32), axis=0),
                    y_out[:, u, :], None, bounds_check=SLOTS - 1, oob_is_err=False).then_inc(y_sent[u], 16)

        @block.tensor
        def _(pe):
            pe.wait_ge(consts, 1)
            pe.wait_ge(par_loaded, 16 * 4)
            nc.tensor.transpose(bank[7][:, 0:P], w_nat[:], ident[:]).then_inc(wt_psum, 1)

            def support_transpose(i):
                pe.wait_ge(xn_ready, i + 1)
                if i >= 2:
                    pe.wait_ge(xnt_ready, i - 1)
                nc.tensor.transpose(bank[5 + i % 2][:, 0:P], support[:, i, :], ident[:]).then_inc(xnt_psum, 1)

            def support_product(i):
                pe.wait_ge(xnt_ready, i + 1)
                if i == 0:
                    pe.wait_ge(wt_ready, 1)
                    pe.wait_ge(consts, 3)
                else:
                    pe.wait_ge(sup_ready, i)
                nc.tensor.matmul(bank[7][:, 0:D], xn_t[:, i % 2, :], w_t[:], start=True, stop=False)
                nc.tensor.matmul(bank[7][:, 0:D], ones_row[:], b_row[:], start=False, stop=True).then_inc(sup_psum, 1)

            support_transpose(0)
            for i in range(NT):
                if i + 1 < NT:
                    support_transpose(i + 1)
                support_product(i)

            blocks = adjT[:].rearrange("p (i j n) -> p i j n", i=NT, j=NT)

            def transpose_rows(k, u, q, first=False):
                pe.wait_ge(a_loaded[u], 16 * (q + 1))
                for g in range(GROUPS):
                    if not first:
                        pe.wait_ge(copied, (k - 1) * GROUPS + g + 1)
                    for j in range(BLOCKS):
                        at = (g * BLOCKS + j) * P
                        mm = nc.tensor.transpose(bank[g][:, j * P:(j + 1) * P], a_rows[:, u, at:at + P], ident[:])
                    mm.then_inc(transposed, 1)

            def eager(j, u, start=False, stop=False):
                pe.wait_ge(scale_step, 3 * j + 2)
                mm = nc.tensor.matmul(bank[4][:], scaled_now[:, u, :], blocks[:, 0:EAGER, j, :],
                                      start=start, stop=stop)
                if stop:
                    mm.then_inc(eager_done, 1)

            def eager_at(j, u):
                pe.wait_ge(scale_step, 3 * j + 2)
                v = adjT[:, 0:EAGER * N].rearrange("p (i m) -> p i m", i=EAGER)
                nc.tensor.matmul(bank[4][:], scaled_now[:, u, :], v[:, :, bass.ds(j * P, P)],
                                 start=False, stop=False)

            for k in range(RING):
                transpose_rows(k, k, 0, first=k == 0)
            pe.wait_ge(copied, RING * GROUPS)
            for j in range(RING - 1):
                eager(j, j, start=j == 0)
            with pe.Fori(0, NT // RING - 1) as r:
                for u in range(RING):
                    transpose_rows(RING * r + (RING + u), u, r + 1)
                    eager_at(RING * r + (RING + u - 1), (u - 1) % RING)
            eager(NT - 1, RING - 1, stop=True)

            def gather(c, lo, hi):
                acc = bank[c % 2]
                if lo == 0 and c >= 4:
                    pe.wait_ge(acc_copied, c - 1)
                for j in range(lo, hi):
                    mm = nc.tensor.matmul(acc[:, 0:2 * P], scaled[:, j, :], blocks[:, 2 * c:2 * c + 2, j, :],
                                          start=j == 0, stop=j == NT - 1)
                if hi == NT:
                    mm.then_inc(acc_done, 1)

            def back(c):
                pe.wait_ge(acc_copied, c + 1)
                for t in range(2):
                    mm = nc.tensor.transpose(bank[2][:, t * P:(t + 1) * P], acc_sb[:, c % 2, t, :], ident[:])
                mm.then_inc(back_psum, 1)

            def turn_rows(c):
                pe.wait_ge(rows_ready, c + 1)
                for t in range(2):
                    mm = nc.tensor.transpose(bank[3][:, t * P:(t + 1) * P], rows[:, c % 2, t, 0, 0:D], ident[:])
                mm.then_inc(rowsT_psum, 1)

            def logits(c):
                pe.wait_ge(rowsT_ready, c + 1)
                for t in range(2):
                    o = bank[5][:, t * E:(t + 1) * E]
                    nc.tensor.matmul(o, xT2[:, c % 2, t, :], gate_sb[:], start=True, stop=False)
                    mm = nc.tensor.matmul(o, ones_row[:], gate_b_row[:], start=False, stop=True)
                mm.then_inc(logits_psum, 1)

            def ranks(c):
                pe.wait_ge(member_ready, c + 1)
                if c:
                    pe.wait_ge(members_ready, 2 * c)
                for t in range(2):
                    o = bank[6][:, t * E:(t + 1) * E]
                    nc.tensor.matmul(o, ones_row[:], region_row[:], start=True, stop=False)
                    nc.tensor.matmul(o, ones[:], members[:, c % 2, :], start=False, stop=False)
                    if t:
                        nc.tensor.matmul(o, ones[:], member[:, c % 2, 0, :], start=False, stop=False)
                    mm = nc.tensor.matmul(o, before[:], member[:, c % 2, t, :], start=False, stop=True)
                mm.then_inc(rank_psum, 1)

            pe.wait_ge(scale_step, 3 * NT)
            pe.wait_ge(consts, NCONST)
            back(0)
            gather(2, 0, 4)
            turn_rows(0)
            gather(2, 4, 6)
            logits(0)
            gather(2, 6, 8)
            back(1)
            ranks(0)
            gather(2, 8, 12)
            turn_rows(1)
            gather(2, 12, 14)
            logits(1)
            gather(2, 14, 16)
            for c in range(2, NPAIR - 1):
                back(c)
                ranks(c - 1)
                gather(c + 1, 0, 7)
                turn_rows(c)
                gather(c + 1, 7, 11)
                logits(c)
                gather(c + 1, 11, NT)
            back(NPAIR - 1)
            ranks(NPAIR - 2)
            turn_rows(NPAIR - 1)
            logits(NPAIR - 1)
            ranks(NPAIR - 1)

            pe.wait_ge(members_ready, 2 * NPAIR)
            nc.tensor.matmul(bank[4][0:NTP, 0:E], ones[:, 0:NTP], members[:, NPAIR % 2, :],
                             start=True, stop=True).then_inc(count_psum, 1)
            pe.wait_ge(tab_step, 14)
            for n in range(2):
                mm = nc.tensor.matmul(bank[7][0:1, n * NTP:(n + 1) * NTP], table_col[:, n:n + 1],
                                      ident[0:NTP, 0:NTP], start=True, stop=True)
            mm.then_inc(tab_psum, 1)

            pe.wait_ge(table_ready, 1)
            pe.wait_ge(w_loaded, 16 * 4)

            def step(s, u, q, stages):
                if 0 in stages:
                    pe.wait_ge(xg_loaded[u], 16 * (q + 1))
                    nc.tensor.transpose(bank[u % 2][:, 0:P], xg[:, u, 0:D], ident[:]).then_inc(xgT_psum, 1)
                if 1 in stages:
                    v = (u - 1) % 2
                    ex = pe.value_load(table[0:1, bass.ds(s - 1 + NTP, 1)], min_val=0, max_val=E - 1)
                    pe.wait_ge(xgT_ready, s)
                    nc.tensor.matmul(bank[2 + v][:], xgT[:, v, :], w12[:, bass.ds(ex * BANK, BANK)],
                                     start=True, stop=True).then_inc(h_psum, 1)
                if 2 in stages:
                    v = u % 2
                    pe.wait_ge(hid_ready, s - 1)
                    for c in range(HC):
                        mm = nc.tensor.transpose(bank[4 + v][:, c * P:(c + 1) * P], hid[:, v, c * P:(c + 1) * P],
                                                 ident[:])
                    mm.then_inc(hidT_psum, 1)
                if 3 in stages:
                    v = (u - 3) % 2
                    ex = pe.value_load(table[0:1, bass.ds(s - 3 + NTP, 1)], min_val=0, max_val=E - 1)
                    pe.wait_ge(hidT_ready, s - 2)
                    if not isinstance(s, int) or s >= 5:
                        pe.wait_ge(y_ready, s - 4)
                    for c in range(HC):
                        mm = nc.tensor.matmul(bank[6 + v][:, 0:D], hidT[:, v, c * P:(c + 1) * P],
                                              w3s[:, bass.ds(ex * HID + c * D, D)], start=c == 0, stop=c == HC - 1)
                    mm.then_inc(y_psum, 1)

            steps(pe, step)

        @block.scalar
        def _(act):
            act.wait_ge(wt_psum, 1)
            nc.scalar.copy(w_t[:], bank[7][:, 0:P]).then_inc(wt_ready, 1)
            for i in range(NT + 1):
                if i < NT:
                    act.wait_ge(xnt_psum, i + 1)
                    if i >= 2:
                        act.wait_ge(sup_psum, i - 1)
                    nc.scalar.copy(xn_t[:, i % 2, :], bank[5 + i % 2][:, 0:P]).then_inc(xnt_ready, 1)
                if i:
                    act.wait_ge(sup_psum, i)
                    nc.scalar.copy(support[:, i - 1, :], bank[7][:, 0:D]).then_inc(sup_ready, 1)

            def copy_rows(k):
                for g in range(GROUPS):
                    act.wait_ge(transposed, k * GROUPS + g + 1)
                    nc.scalar.copy(adjT[:, bass.ds(k * N + g * BANK, BANK)], bank[g][:]).then_inc(copied, 1)

            with act.Fori(0, NT) as k:
                copy_rows(k)

            def copy_acc(c):
                if c >= 2:
                    act.wait_ge(back_psum, c - 1)
                if c < 2:
                    act.wait_ge(eager_done, 1)
                    src = bank[4][:, c * 2 * P:(c + 1) * 2 * P]
                else:
                    act.wait_ge(acc_done, c - 1)
                    src = bank[c % 2][:, 0:2 * P]
                nc.scalar.copy(acc_sb[:, c % 2].rearrange("p t n -> p (t n)"), src).then_inc(acc_copied, 1)

            def route(c):
                if c >= 2:
                    act.wait_ge(rows_sent[c % 2], 16 * 2 * TOPK * (c // 2))
                nc.scalar.copy(rows[:, c % 2, :, :, D + 1].bitcast(I32), dest[:, 2 * c:2 * c + 2, :]).then_inc(dest_ready, 1)
                act.wait_ge(rowsT_psum, c + 1)
                nc.scalar.copy(xT2[:, c % 2].rearrange("p t n -> p (t n)"), bank[3][:, 0:2 * P]).then_inc(rowsT_ready, 1)
                act.wait_ge(gap_ready, c + 1)
                nc.scalar.activation(e_gap[:], gap[:], ACT.Exp).then_inc(e_ready, 1)

            act.wait_ge(consts, NCONST)
            copy_acc(0)
            copy_acc(1)
            for c in range(NPAIR):
                route(c)
                if c >= 1 and c + 1 < NPAIR:
                    copy_acc(c + 1)

            def step(s, u, q, stages):
                if 1 in stages:
                    v = (u - 1) % 2
                    act.wait_ge(h_psum, s)
                    nc.scalar.activation(sil[:, v, :], bank[2 + v][:, 0:HID], ACT.Silu).then_inc(sil_ready, 1)
                if 2 in stages:
                    v = u % 2
                    act.wait_ge(hidT_psum, s - 1)
                    nc.scalar.copy(hidT[:, v, :], bank[4 + v][:, 0:HID]).then_inc(hidT_ready, 1)

            steps(act, step)

        @block.vector
        def _(dve):
            dve.wait_ge(x_loaded, 16)
            for i in range(NT):
                nc.vector.bn_stats(x_stats[:, i, :], x_mid[:, i, :]).then_inc(x_stat, 1)
            for i in range(NT):
                dve.wait_ge(x_stat, i + 1)
                nc.vector.bn_aggr(x_mv[:, i, :], x_stats[:, i, :]).then_inc(x_stat, 1)
            dve.wait_ge(x_stat, 2 * NT)
            nc.vector.tensor_scalar(x_var[:], x_mv[:, :, 1], EPS, None, ALU.add).then_inc(x_var_ready, 1)
            dve.wait_ge(x_rstd_ready, 1)
            for i in range(NT):
                nc.vector.tensor_scalar(support[:, i, :], x_mid[:, i, :], x_mv[:, i, 0:1], x_rstd[:, i:i + 1],
                                        ALU.subtract, ALU.mult).then_inc(xn_ready, 1)

            def sum_rows(k, u):
                dve.wait_ge(fold_done, k + 1)
                col = bass.ds(k, 1)
                nc.vector.tensor_reduce(row_sum[:, col], folded[:, u % 2, :], AX_X, ALU.add).then_inc(row_step, 1)
                dve.wait_ge(row_step, 3 * k + 1)
                nc.vector.tensor_scalar(no_degree[:, col], row_sum[:, col], -1.0, None, ALU.is_equal).then_inc(row_step, 1)
                dve.wait_ge(row_step, 3 * k + 2)
                nc.vector.scalar_tensor_tensor(out=degree[:, col], in0=row_sum[:, col], scalar=1.0,
                                               in1=no_degree[:, col], op0=ALU.add, op1=ALU.add).then_inc(row_step, 1)

            def scale_rows(k, u, first=False):
                col = bass.ds(k, 1)
                dve.wait_ge(root_ready, k + 1)
                nc.vector.tensor_tensor(dinv[:, col], root[:, col], no_degree[:, col], ALU.subtract).then_inc(scale_step, 1)
                dve.wait_ge(scale_step, 3 * k + 1)
                if not first:
                    dve.wait_ge(transposed, k * GROUPS + 1)
                nc.vector.tensor_scalar(scaled_now[:, u, :], support[:, bass.ds(k, 1), :].rearrange("p a d -> p (a d)"),
                                        dinv[:, col], None, ALU.mult).then_inc(scale_step, 1)
                dve.wait_ge(scale_step, 3 * k + 2)
                nc.vector.tensor_copy(scaled[:, bass.ds(k, 1), :].rearrange("p a d -> p (a d)"),
                                      scaled_now[:, u, :])
                nc.vector.scalar_tensor_tensor(
                    out=x_mid[:, bass.ds(k, 1), :].rearrange("p a d -> p (a d)"), in0=scaled_now[:, u, :],
                    scalar=dinv[:, col], in1=x_mid[:, bass.ds(k, 1), :].rearrange("p a d -> p (a d)"),
                    op0=ALU.mult, op1=ALU.add).then_inc(scale_step, 1)

            dve.wait_ge(sup_ready, NT)
            for k in range(RING):
                sum_rows(k, k)
                if k:
                    scale_rows(k - 1, k - 1, first=True)
            with dve.Fori(0, NT // RING - 1) as r:
                for u in range(RING):
                    sum_rows(RING * r + (RING + u), u)
                    k = RING * r + (RING + u - 1)
                    scale_rows(k, (u - 1) % RING)
            scale_rows(NT - 1, RING - 1)

            def mix(c):
                dve.wait_ge(back_psum, c + 1)
                for t in range(2):
                    i = 2 * c + t
                    nc.vector.scalar_tensor_tensor(out=x_mid[:, i, :], in0=bank[2][:, t * P:(t + 1) * P],
                                                   scalar=dinv[:, i:i + 1], in1=x_mid[:, i, :],
                                                   op0=ALU.mult, op1=ALU.add).then_inc(mix_step, 1)
                for t in range(2):
                    dve.wait_ge(mix_step, 6 * c + 1 + t)
                    nc.vector.bn_stats(stats[:, t, :], x_mid[:, 2 * c + t, :]).then_inc(mix_step, 1)
                for t in range(2):
                    dve.wait_ge(mix_step, 6 * c + 3 + t)
                    nc.vector.bn_aggr(mv[:, t, :], stats[:, t, :]).then_inc(mix_step, 1)
                dve.wait_ge(mix_step, 6 * c + 6)
                nc.vector.tensor_scalar(var[:], mv[:, :, 1], EPS, None, ALU.add).then_inc(var_ready, 1)

            def fill_rows(c):
                dve.wait_ge(rstd_ready, c + 1)
                if c >= 2:
                    dve.wait_ge(rows_sent[c % 2], 16 * 2 * TOPK * (c // 2))
                for k in range(TOPK):
                    for t in range(2):
                        v = nc.vector.tensor_scalar(rows[:, c % 2, t, k, 0:D], x_mid[:, 2 * c + t, :], mv[:, t, 0:1],
                                                    rstd[:, t:t + 1], ALU.subtract, ALU.mult)
                    if k == 0:
                        v.then_inc(rows_ready, 1)

            def choose(c):
                at = 6 * c
                dve.wait_ge(logits_psum, c + 1)
                for t in range(2):
                    nc.vector.max(best[:, t, :], bank[5][:, t * E:(t + 1) * E]).then_inc(pick_step, 1)
                dve.wait_ge(pick_step, at + 2)
                nc.vector.tensor_tensor(gap[:], best[:, :, 1], best[:, :, 0], ALU.subtract).then_inc(gap_ready, 1)
                for t in range(2):
                    v = nc.vector.max_index(best_at[:, t, :], best[:, t, :], bank[5][:, t * E:(t + 1) * E])
                v.then_inc(pick_step, 1)
                dve.wait_ge(pick_step, at + 3)
                for k in range(TOPK):
                    v = nc.vector.tensor_tensor(chosen[:, k], iota_e[:].unsqueeze(1).to_broadcast([P, 2, E]),
                                                best_at[:, :, k:k + 1].to_broadcast([P, 2, E]), ALU.is_equal)
                v.then_inc(pick_step, 1)
                dve.wait_ge(pick_step, at + 4)
                nc.vector.tensor_tensor(member[:, c % 2], chosen[:, 0], chosen[:, 1], ALU.add).then_inc(member_ready, 1)
                dve.wait_ge(member_ready, c + 1)
                nc.vector.tensor_tensor(members[:, 2, :], members[:, c % 2, :], member[:, c % 2, 0, :],
                                        ALU.add).then_inc(members_ready, 1)
                dve.wait_ge(members_ready, 2 * c + 1)
                nc.vector.tensor_tensor(members[:, (c + 1) % 2, :], members[:, 2, :], member[:, c % 2, 1, :],
                                        ALU.add).then_inc(members_ready, 1)
                dve.wait_ge(e_ready, c + 1)
                nc.vector.tensor_scalar(e_sum[:], e_gap[:], 1.0, None, ALU.add).then_inc(pick_step, 1)
                dve.wait_ge(pick_step, at + 5)
                nc.vector.reciprocal(rows[:, c % 2, :, 0, D], e_sum[:]).then_inc(pick_step, 1)

            def place(c):
                dve.wait_ge(pick_step, 6 * c + 6)
                nc.vector.tensor_tensor(rows[:, c % 2, :, 1, D], e_gap[:], rows[:, c % 2, :, 0, D], ALU.mult)
                dve.wait_ge(rank_psum, c + 1)
                for k in range(TOPK):
                    v = nc.vector.tensor_tensor(picked[:, k], chosen[:, k],
                                                bank[6][:, 0:2 * E].rearrange("p (t e) -> p t e", t=2), ALU.mult)
                v.then_inc(gate_step, 1)
                dve.wait_ge(gate_step, 2 * c + 1)
                nc.vector.tensor_reduce(slot_f[:], picked[:], AX_X, ALU.add).then_inc(gate_step, 1)
                dve.wait_ge(gate_step, 2 * c + 2)
                nc.vector.tensor_copy(slot[:, c % 2], slot_f[:]).then_inc(slot_ready, 1)

            dve.wait_ge(consts, NCONST)
            dve.wait_ge(scale_step, 3 * NT)
            for c in range(NPAIR):
                mix(c)
                if c:
                    place(c - 1)
                fill_rows(c)
                choose(c)
            place(NPAIR - 1)

            chain = [0]

            def link(v):
                chain[0] += 1
                v.then_inc(tab_step, 1)
                dve.wait_ge(tab_step, chain[0])

            dve.wait_ge(count_psum, 1)
            link(nc.vector.tensor_copy(cnt[:], bank[4][0:NTP, 0:E]))
            link(nc.vector.tensor_scalar(cnt_up[:], cnt[:], float(P - 1), None, ALU.add))
            link(nc.vector.tensor_scalar(tiles_i[:], cnt_up[:], P.bit_length() - 1, None, ALU.arith_shift_right))
            link(nc.vector.tensor_copy(tiles_f[:], tiles_i[:]))
            link(nc.vector.tensor_tensor_scan(upto[:], tiles_f[:], zeros_e[:], 0.0, ALU.add, ALU.add))
            link(nc.vector.tensor_tensor(prior[:], upto[:], tiles_f[:], ALU.subtract))
            link(nc.vector.scalar_tensor_tensor(out=end_row[:], in0=prior[:], scalar=float(P), in1=cnt[:],
                                                op0=ALU.mult, op1=ALU.add))
            link(nc.vector.tensor_tensor(end_row[:], end_row[:], region_col[:], ALU.add))
            link(nc.vector.tensor_scalar(passed[:], upto[:], tile_no[:], 0.0, ALU.is_le, ALU.add, accum_out=n_passed[:]))
            link(nc.vector.scalar_tensor_tensor(out=is_own[:], in0=prior[:], scalar=tile_no[:], in1=passed[:],
                                                op0=ALU.is_le, op1=ALU.subtract))
            link(nc.vector.scalar_tensor_tensor(out=end_row[:], in0=is_own[:], scalar=1.0, in1=end_row[:],
                                                op0=ALU.mult, op1=ALU.mult, accum_out=start_sum[:]))
            link(nc.vector.tensor_scalar(live[:], n_passed[:], float(E), None, ALU.is_lt))
            link(nc.vector.tensor_scalar(start_sum[:], start_sum[:], tile_row[:], float(-NULL_ROW), ALU.subtract, ALU.add))
            nc.vector.tensor_scalar(table_col[:, 0:1], start_sum[:], live[:], float(NULL_ROW), ALU.mult, ALU.add)
            nc.vector.tensor_scalar(table_col[:, 1:2], n_passed[:], float(E - 1), None, ALU.min).then_inc(tab_step, 1)
            dve.wait_ge(tab_psum, 1)
            nc.vector.tensor_copy(table[:], bank[7][0:1, 0:2 * NTP]).then_inc(table_ready, 1)

            def step(s, u, q, stages):
                if 0 in stages:
                    dve.wait_ge(xgT_psum, s + 1)
                    nc.vector.tensor_copy(xgT[:, u % 2, :], bank[u % 2][:, 0:P]).then_inc(xgT_ready, 1)
                    dve.wait_ge(xg_loaded[u], 16 * (q + 1))
                    if not isinstance(s, int) or s >= RING:
                        dve.wait_ge(y_ready, s - LAG)
                    nc.vector.tensor_copy(meta[:, u, :], xg[:, u, D:ROW]).then_inc(meta_ready, 1)
                if 1 in stages:
                    v = (u - 1) % 2
                    dve.wait_ge(sil_ready, s)
                    nc.vector.tensor_tensor(hid[:, v, :], sil[:, v, :], bank[2 + v][:, HID:BANK],
                                            ALU.mult).then_inc(hid_ready, 1)
                if 3 in stages:
                    v, w = (u - 3) % 2, (u - 3) % RING
                    dve.wait_ge(y_psum, s - 2)
                    if not isinstance(s, int) or s - LAG >= RING:
                        dve.wait_ge(y_sent[w], 16 * (q_of(s, q, u)))
                    dve.wait_ge(meta_ready, s - 2)
                    nc.vector.tensor_copy(y_dest[:, w, :], meta[:, w, 1:2])
                    nc.vector.tensor_scalar(y_out[:, w, :], bank[6 + v][:, 0:D], meta[:, w, 0:1], None,
                                            ALU.mult).then_inc(y_ready, 1)

            def q_of(s, q, u):
                return q - (1 if u < LAG else 0)

            steps(dve, step)

            per = NT // RING
            for q in range(RING):
                part = slice(q * per, (q + 1) * per)
                dve.wait_ge(z_loaded[q], 16)
                nc.vector.tensor_tensor(z_buf[:, part, 0, :], z_buf[:, part, 0, :], z_buf[:, part, 1, :],
                                        ALU.add).then_inc(z_sum, 1)
                dve.wait_ge(z_sum, q + 1)
                nc.vector.tensor_tensor(x_mid[:, part, :], x_mid[:, part, :], z_buf[:, part, 0, :],
                                        ALU.add).then_inc(out_ready, 1)


_INS = ["x", "adj", "L0_gnn_W", "L0_gnn_b", "L0_ffn_gate_w", "L0_ffn_gate_b", "L0_ffn_w1", "L0_ffn_w2", "L0_ffn_w3"]


def kernel(**inputs):
    import concourse.bacc as bacc
    from concourse.bass_utils import run_bass_kernel_spmd

    nc = bacc.Bacc("TRN2", target_bir_lowering=False, num_devices=1)
    arrays, args = {}, []
    for name in _INS:
        a = np.ascontiguousarray(inputs[name])
        arrays[f"in_{name}"] = a
        args.append(nc.dram_tensor(f"in_{name}", a.shape, mybir.dt.from_np(a.dtype), kind="ExternalInput").ap())
    out = nc.dram_tensor("out", inputs["x"].shape, F32, kind="ExternalOutput").ap()
    graph_moe(nc, *args, out)
    r = run_bass_kernel_spmd(nc, [arrays], core_ids=[0])
    return r.results[0]["out"]
```

```python
from contextlib import ExitStack
from itertools import count

import numpy as np

import concourse.bass as bass
from concourse import mybir

F32 = mybir.dt.float32
BF16 = mybir.dt.bfloat16
I32 = mybir.dt.int32
U32 = mybir.dt.uint32
ALU = mybir.AluOpType
ACT = mybir.ActivationFunctionType
AX_X = mybir.AxisListType.X

P = 128
BANK = 512
EPS = 1e-5


def graph_moe(nc, x, adj, w_gnn, b_gnn, gate_w, gate_b, w1, w2, w3, out):
    N, D = x.shape
    E, _, HID = w1.shape
    NT = N // P
    TOPK = 2
    RING = 4
    EAGER = BANK // P
    NPAIR = NT // 2
    XG = BANK // D
    NXG = NT // XG
    BLOCKS = BANK // P
    GROUPS = NT // BLOCKS
    HALF = N // 2
    HC = HID // P
    REGION = P + N
    NULL_ROW = E * REGION
    SLOTS = TOPK * N
    NTILE = SLOTS // P + E - 1
    ROW = D + 2
    NTP = NTILE + 1
    assert D == P and HC == 2 and 2 * HID == BANK and NT % RING == 0 and EAGER == RING

    with ExitStack() as ctx:
        def sb(name, shape, dtype=F32):
            return ctx.enter_context(nc.sbuf_tensor(name, shape, dtype))

        def sem(name):
            return ctx.enter_context(nc.semaphore(name))

        x_sorted = nc.dram_tensor("x_sorted", [NULL_ROW + P, ROW], F32, kind="Internal").ap()
        y_tokens = nc.dram_tensor("y_tokens", [SLOTS, D], F32, kind="Internal").ap()

        adjT = sb("adjT", [P, NT * N])
        a_rows = sb("a_rows", [P, RING, N])
        folded = sb("folded", [P, 2, HALF])
        x_mid = sb("x_mid", [P, NT, D])
        support = sb("support", [P, NT, D])
        scaled = sb("scaled", [P, NT, D])
        scaled_now = sb("scaled_now", [P, RING, D])
        w_nat = sb("w_nat", [P, D])
        w_t = sb("w_t", [P, D])
        b_row = sb("b_row", [1, D])
        gate_sb = sb("gate_sb", [P, E])
        gate_b_row = sb("gate_b_row", [1, E])
        ident = sb("ident", [P, P])
        ones_row = sb("ones_row", [1, P])
        before = sb("before", [P, P], BF16)
        ones = sb("ones", [P, P], BF16)
        iota_e = sb("iota_e", [P, E])
        region_row = sb("region_row", [1, E])
        region_col = sb("region_col", [NTP, E])
        tile_no = sb("tile_no", [NTP, 1])
        tile_row = sb("tile_row", [NTP, 1])
        dest = sb("dest", [P, NT, TOPK], I32)
        minus_half = sb("minus_half", [P, NT])
        pad = sb("pad", [P, ROW])
        xn_t = sb("xn_t", [P, 2, XG * D])
        b_all = sb("b_all", [P, D])
        x_stats = sb("x_stats", [P, NT, 6])
        x_mv = sb("x_mv", [P, NT, 2])
        x_var = sb("x_var", [P, NT])
        x_rstd = sb("x_rstd", [P, NT])
        row_sum = sb("row_sum", [P, NT])
        no_degree = sb("no_degree", [P, NT])
        degree = sb("degree", [P, NT])
        root = sb("root", [P, NT])
        dinv = sb("dinv", [P, NT])
        stats = sb("stats", [P, 2, 6])
        mv = sb("mv", [P, 2, 2])
        var = sb("var", [P, 2])
        rstd = sb("rstd", [P, 2])
        best = sb("best", [P, 2, 8])
        best_at = sb("best_at", [P, 2, 8], U32)
        gap = sb("gap", [P, 2])
        e_gap = sb("e_gap", [P, 2])
        e_sum = sb("e_sum", [P, 2])
        chosen = sb("chosen", [P, TOPK, 2, E])
        member = sb("member", [P, 2, 2, E], BF16)
        members = sb("members", [P, 3, E], BF16)
        picked = sb("picked", [P, TOPK, 2, E])
        slot_f = sb("slot_f", [P, TOPK, 2])
        slot = sb("slot", [P, 2, TOPK, 2], U32)
        cnt = sb("cnt", [NTP, E])
        cnt_up = sb("cnt_up", [NTP, E], I32)
        tiles_i = sb("tiles_i", [NTP, E], I32)
        tiles_f = sb("tiles_f", [NTP, E])
        zeros_e = sb("zeros_e", [NTP, E])
        upto = sb("upto", [NTP, E])
        prior = sb("prior", [NTP, E])
        end_row = sb("end_row", [NTP, E])
        passed = sb("passed", [NTP, E])
        is_own = sb("is_own", [NTP, E])
        n_passed = sb("n_passed", [NTP, 1])
        live = sb("live", [NTP, 1])
        start_sum = sb("start_sum", [NTP, 1])
        table_col = sb("table_col", [NTP, 2])
        table = sb("table", [1, 2 * NTP], I32)
        meta = sb("meta", [P, RING, 2])
        y_dest = sb("y_dest", [P, RING, 1])

        WROW = BANK + HID
        w_all = adjT[:, 0:E * WROW]
        z_at = 8 * N
        z_buf = adjT[:, z_at:z_at + NT * TOPK * D].rearrange("p (i k d) -> p i k d", k=TOPK, d=D)

        late = a_rows[:].rearrange("p u n -> p (u n)")
        used = 0

        def over(shape, pattern=None, **sizes):
            nonlocal used
            n = int(np.prod(shape))
            part = late[:, used:used + n]
            used += n
            return part.rearrange(pattern, **sizes) if pattern else part

        acc_sb = over([2, 2, P], "p (c t n) -> p c t n", c=2, t=2)
        rows = over([2, 2, TOPK, ROW], "p (c t k n) -> p c t k n", c=2, t=2, k=TOPK)
        xT2 = over([2, 2, P], "p (c t n) -> p c t n", c=2, t=2)
        xg = over([RING, ROW], "p (u n) -> p u n", u=RING)
        xgT = over([2, P], "p (u n) -> p u n", u=2)
        sil = over([2, HID], "p (u n) -> p u n", u=2)
        hid = over([2, HID], "p (u n) -> p u n", u=2)
        hidT = over([2, HID], "p (u n) -> p u n", u=2)
        y_out = over([RING, D], "p (u n) -> p u n", u=RING)
        assert used <= RING * N

        bank = [ctx.enter_context(nc.psum_tensor(f"bank{i}", [P, BANK], F32)) for i in range(8)]

        consts = sem("consts")
        fill = sem("fill")
        x_loaded = [sem(f"x_loaded{i}") for i in range(NXG)]
        par_loaded = sem("par_loaded")
        a_loaded = [sem(f"a_loaded{i}") for i in range(RING)]
        x_stat = sem("x_stat")
        x_var_ready = sem("x_var_ready")
        x_rstd_ready = sem("x_rstd_ready")
        xn_ready = sem("xn_ready")
        wb_psum = sem("wb_psum")
        wb_ready = sem("wb_ready")
        xnt_psum = sem("xnt_psum")
        xnt_ready = sem("xnt_ready")
        sup_psum = sem("sup_psum")
        sup_ready = sem("sup_ready")
        transposed = sem("transposed")
        copied = sem("copied")
        fold_done = sem("fold_done")
        row_step = sem("row_step")
        root_ready = sem("root_ready")
        scale_step = sem("scale_step")
        eager_done = sem("eager_done")
        acc_done = sem("acc_done")
        acc_copied = sem("acc_copied")
        back_psum = sem("back_psum")
        mix_step = sem("mix_step")
        var_ready = sem("var_ready")
        rstd_ready = sem("rstd_ready")
        rows_ready = sem("rows_ready")
        dest_ready = sem("dest_ready")
        rowsT_psum = sem("rowsT_psum")
        rowsT_ready = sem("rowsT_ready")
        logits_psum = sem("logits_psum")
        gap_ready = sem("gap_ready")
        e_ready = sem("e_ready")
        pick_step = sem("pick_step")
        member_ready = sem("member_ready")
        members_ready = sem("members_ready")
        rank_psum = sem("rank_psum")
        gate_step = sem("gate_step")
        slot_ready = sem("slot_ready")
        rows_sent = [sem(f"rows_sent{i}") for i in range(2)]
        pads_sent = sem("pads_sent")
        count_psum = sem("count_psum")
        tab_step = sem("tab_step")
        tab_psum = sem("tab_psum")
        table_ready = sem("table_ready")
        w_loaded = sem("w_loaded")
        xg_loaded = [sem(f"xg_loaded{i}") for i in range(RING)]
        xgT_psum = sem("xgT_psum")
        xgT_ready = sem("xgT_ready")
        meta_ready = sem("meta_ready")
        h_psum = sem("h_psum")
        sil_ready = sem("sil_ready")
        hid_ready = sem("hid_ready")
        hidT_psum = sem("hidT_psum")
        hidT_ready = sem("hidT_ready")
        y_psum = sem("y_psum")
        y_ready = sem("y_ready")
        y_sent = [sem(f"y_sent{i}") for i in range(RING)]
        z_loaded = [sem(f"z_loaded{i}") for i in range(RING)]
        z_sum = sem("z_sum")
        out_ready = sem("out_ready")
        out_sent = sem("out_sent")

        NCONST = 14
        serial = count()

        LAG = 3
        FULL = NTILE - LAG
        assert FULL % RING == 0

        def load_values(eng, first, n, most):
            regs = [eng.alloc_register(f"{eng.engine}_entry{i}_{next(serial)}") for i in range(n)]
            eng.load(regs, table[0:1, bass.ds(first, n)])
            return [eng.snap(reg, min_val=0, max_val=most) for reg in regs]

        def steps(eng, step, load_weight_columns=None):
            load = load_weight_columns or (lambda first, n: None)
            head = LAG + RING
            v = load(0, head - 1)
            for s in range(head):
                step(s, s % RING, s // RING, range(min(s, LAG) + 1), lambda n: v[s - n])
            with eng.Fori(0, FULL // RING - 1) as r:
                v = load(RING * r + RING, RING + LAG - 1)
                for i in range(RING):
                    s = head + i
                    step(RING * r + s, s % RING, r + s // RING, range(LAG + 1), lambda n: v[i + LAG - n])
            v = load(NTILE - LAG, LAG)
            for i in range(LAG):
                s = NTILE + i
                step(s, s % RING, s // RING, range(i + 1, LAG + 1), lambda n: v[i + LAG - n])

        block = ctx.enter_context(nc.Block())

        @block.sync
        def _(sp):
            x_v = x.rearrange("(i p) d -> p i d", p=P)
            for g in range(NXG):
                part = slice(g * XG, (g + 1) * XG)
                sp.dma_start(x_mid[:, part], x_v[:, part]).then_inc(x_loaded[g], 16)

            def load_rows(k, u):
                sp.dma_start(a_rows[:, u, :], adj[bass.ds(k * P, P), :]).then_inc(a_loaded[u], 16)

            for u in range(RING):
                load_rows(u, u)
            with sp.Fori(0, NT // RING - 1) as r:
                for u in range(RING):
                    sp.wait_ge(transposed, (RING * r + u + 1) * GROUPS)
                    if u:
                        sp.wait_ge(fold_done, RING * r + u)
                    else:
                        sp.wait_ge(row_step, 2 * RING * r + 1)
                    load_rows(RING * r + u + RING, u)
            sp.wait_ge(consts, NCONST)
            for e in range(E + 1):
                sp.dma_start(x_sorted[e * REGION:e * REGION + P, :], pad[:]).then_inc(pads_sent, 16)
            sp.wait_ge(eager_done, 1)
            sp.wait_ge(acc_done, 1)
            w_v = w_all.rearrange("p (e n) -> p e n", e=E)
            sp.dma_start(w_v[:, :, 0:HID], w1.rearrange("e d h -> d e h")).then_inc(w_loaded, 16)
            sp.dma_start(w_v[:, :, HID:BANK], w2.rearrange("e d h -> d e h")).then_inc(w_loaded, 16)
            for c in range(HC):
                sp.dma_start(w_v[:, :, BANK + c * D:BANK + (c + 1) * D],
                             w3[:, c * P:(c + 1) * P, :].rearrange("e h d -> h e d")).then_inc(w_loaded, 16)

            for i in range(2):
                sp.wait_ge(rows_sent[i], 16 * 2 * TOPK * NPAIR // 2)
            sp.wait_ge(pads_sent, 16 * (E + 1))
            sp.wait_ge(table_ready, 1)

            def load_tile(first, u):
                sp.dma_start(xg[:, u, :], x_sorted[bass.ds(first, P), :]).then_inc(xg_loaded[u], 16)

            first = load_values(sp, 0, RING, NULL_ROW)
            for t in range(RING):
                load_tile(first[t], t)
            rounds = NTILE // RING
            with sp.Fori(0, rounds - 1) as r:
                first = load_values(sp, RING * r + RING, RING, NULL_ROW)
                for u in range(RING):
                    sp.wait_ge(meta_ready, RING * r + u + 1)
                    load_tile(first[u], u)
            first = load_values(sp, RING * rounds, NTILE - RING * rounds, NULL_ROW)
            for t in range(RING * rounds, NTILE):
                sp.wait_ge(meta_ready, t - RING + 1)
                load_tile(first[t % RING], t % RING)

            for u in range(RING):
                sp.wait_ge(y_sent[u], 16 * len(range(u, NTILE, RING)))
            z_dram = y_tokens.rearrange("(i p k) d -> p i (k d)", p=P, k=TOPK)
            for q in range(RING):
                part = slice(q * NT // RING, (q + 1) * NT // RING)
                sp.dma_start(z_buf[:, part].rearrange("p i k d -> p i (k d)"), z_dram[:, part]).then_inc(z_loaded[q], 16)
            out_v = out.rearrange("(i p) d -> p i d", p=P)
            for q in range(RING):
                part = slice(q * NT // RING, (q + 1) * NT // RING)
                sp.wait_ge(out_ready, q + 1)
                sp.dma_start(out_v[:, part], x_mid[:, part]).then_inc(out_sent, 16)
            sp.wait_ge(out_sent, 16 * RING)

        @block.gpsimd
        def _(pool):
            nc.gpsimd.memset(ident[:], 0.0).then_inc(fill, 1)
            nc.gpsimd.memset(before[:], 1.0).then_inc(fill, 1)
            nc.gpsimd.memset(pad[:], 0.0).then_inc(fill, 1)
            pool.wait_ge(fill, 3)
            nc.gpsimd.affine_select(out=ident[:], in_=ident[:], compare_op=ALU.not_equal, fill=1.0, base=0,
                                    pattern=[[-1, P]], channel_multiplier=1).then_inc(consts, 1)
            nc.gpsimd.memset(minus_half[:], -0.5).then_inc(consts, 1)
            nc.gpsimd.memset(ones_row[:], 1.0).then_inc(consts, 1)
            nc.gpsimd.affine_select(out=before[:], in_=before[:], compare_op=ALU.is_gt, fill=0.0, base=0,
                                    pattern=[[1, P]], channel_multiplier=-1).then_inc(consts, 1)
            nc.gpsimd.memset(ones[:], 1.0).then_inc(consts, 1)
            nc.gpsimd.memset(members[:], 0.0).then_inc(consts, 1)
            nc.gpsimd.memset(zeros_e[:], 0.0).then_inc(consts, 1)
            exact = dict(allow_small_or_imprecise_dtypes=True)
            nc.gpsimd.iota(iota_e[:], pattern=[[1, E]], base=0, channel_multiplier=0, **exact).then_inc(consts, 1)
            nc.gpsimd.iota(region_row[:], pattern=[[REGION, E]], base=P, channel_multiplier=0, **exact).then_inc(consts, 1)
            nc.gpsimd.iota(region_col[:], pattern=[[REGION, E]], base=0, channel_multiplier=0, **exact).then_inc(consts, 1)
            nc.gpsimd.iota(tile_no[:], pattern=[[0, 1]], base=0, channel_multiplier=1, **exact).then_inc(consts, 1)
            nc.gpsimd.iota(tile_row[:], pattern=[[0, 1]], base=0, channel_multiplier=P, **exact).then_inc(consts, 1)
            nc.gpsimd.iota(dest[:], pattern=[[TOPK * P, NT], [1, TOPK]], base=0, channel_multiplier=TOPK).then_inc(consts, 1)
            nc.gpsimd.iota(pad[:, D + 1:ROW].bitcast(I32), pattern=[[0, 1]], base=SLOTS, channel_multiplier=0).then_inc(consts, 1)

            def x_root(g):
                pool.wait_ge(x_var_ready, g + 1)
                part = slice(g * XG, (g + 1) * XG)
                nc.gpsimd.tensor_tensor(x_rstd[:, part], x_var[:, part], minus_half[:, part],
                                        ALU.pow).then_inc(x_rstd_ready, 1)

            def fold(k, u, q, first=False):
                pool.wait_ge(a_loaded[u], 16 * (q + 1))
                if not first:
                    pool.wait_ge(row_step, 2 * k - 3 - u % 2)
                nc.gpsimd.tensor_tensor(folded[:, u % 2, :], a_rows[:, u, 0:HALF], a_rows[:, u, HALF:N],
                                        ALU.add).then_inc(fold_done, 1)

            def take_root(c):
                pool.wait_ge(row_step, 4 * c + 4)
                nc.gpsimd.tensor_tensor(root[:, bass.ds(2 * c, 2)], degree[:, bass.ds(2 * c, 2)],
                                        minus_half[:, 0:2], ALU.pow).then_inc(root_ready, 1)

            pool.wait_ge(consts, 2)
            for g in range(NXG):
                x_root(g)
            fold(1, 1, 0, first=True)
            fold(2, 2, 0, first=True)
            take_root(0)
            fold(3, 3, 0)
            with pool.Fori(0, NT // RING - 1) as r:
                for u in range(0, RING, 2):
                    fold(RING * r + (RING + u), u, r + 1)
                    take_root(2 * r + (1 + u // 2))
                    fold(RING * r + (RING + u + 1), u + 1, r + 1)
            take_root(NPAIR - 1)

            def pair_root(c):
                pool.wait_ge(var_ready, c + 1)
                nc.gpsimd.tensor_tensor(rstd[:], var[:], minus_half[:, 0:2], ALU.pow).then_inc(rstd_ready, 1)

            def send_rows(c, u):
                pool.wait_ge(slot_ready, c + 1)
                pool.wait_ge(dest_ready, c + 1)
                for t in range(2):
                    for k in range(TOPK):
                        nc.gpsimd.indirect_dma_start(
                            x_sorted, bass.IndirectOffsetOnAxis(ap=slot[:, u, k, t:t + 1], axis=0),
                            rows[:, u, t, k, :], None).then_inc(rows_sent[u], 16)

            pair_root(0)
            for c in range(NPAIR):
                if c + 1 < NPAIR:
                    pair_root(c + 1)
                send_rows(c, c % 2)

            for t in range(NTILE):
                u = t % RING
                pool.wait_ge(y_ready, t + 1)
                nc.gpsimd.indirect_dma_start(
                    y_tokens, bass.IndirectOffsetOnAxis(ap=y_dest[:, u, :].bitcast(U32), axis=0),
                    y_out[:, u, :], None, bounds_check=SLOTS - 1, oob_is_err=False).then_inc(y_sent[u], 16)

        @block.tensor
        def _(pe):
            pe.wait_ge(consts, 3)
            pe.wait_ge(par_loaded, 16 * 4)
            nc.tensor.transpose(bank[4][:, 0:P], w_nat[:], ident[:])
            nc.tensor.matmul(bank[4][:, P:P + D], ones_row[:], b_row[:], start=True, stop=True).then_inc(wb_psum, 1)

            def support_transpose(g):
                pe.wait_ge(xn_ready, (g + 1) * XG)
                if g >= 2:
                    pe.wait_ge(xnt_ready, g - 1)
                for i in range(XG):
                    mm = nc.tensor.transpose(bank[5 + g % 2][:, i * P:(i + 1) * P], support[:, g * XG + i, :], ident[:])
                mm.then_inc(xnt_psum, 1)

            def support_product(g):
                pe.wait_ge(xnt_ready, g + 1)
                if g == 0:
                    pe.wait_ge(wb_ready, 2)
                else:
                    pe.wait_ge(sup_ready, g)
                for i in range(XG):
                    mm = nc.tensor.matmul(bank[7][:, i * D:(i + 1) * D], xn_t[:, g % 2, i * P:(i + 1) * P], w_t[:],
                                          start=True, stop=True)
                mm.then_inc(sup_psum, 1)

            blocks = adjT[:].rearrange("p (i j n) -> p i j n", i=NT, j=NT)

            def transpose_rows(k, u, q, first=False):
                pe.wait_ge(a_loaded[u], 16 * (q + 1))
                for g in range(GROUPS):
                    if not first:
                        pe.wait_ge(copied, (k - 1) * GROUPS + g + 1)
                    for j in range(BLOCKS):
                        at = (g * BLOCKS + j) * P
                        mm = nc.tensor.transpose(bank[g][:, j * P:(j + 1) * P], a_rows[:, u, at:at + P], ident[:])
                    mm.then_inc(transposed, 1)

            def eager(c, h, start=False, stop=False):
                pe.wait_ge(scale_step, 3 * c + 2)
                v = adjT[:, 0:EAGER * N].rearrange("p (i m) -> p i m", i=EAGER)
                for t in range(2):
                    mm = nc.tensor.matmul(bank[4][:], scaled_now[:, 2 * h + t, :],
                                          v[:, :, bass.ds(c * 2 * P + t * P, P)],
                                          start=start and t == 0, stop=stop and t == 1)
                if stop:
                    mm.then_inc(eager_done, 1)

            support_transpose(0)
            for k in range(RING):
                transpose_rows(k, k, 0, first=k == 0)
                if k + 1 < NXG:
                    support_transpose(k + 1)
                support_product(k)
            pe.wait_ge(copied, RING * GROUPS)
            eager(0, 0, start=True)
            with pe.Fori(0, NT // RING - 1) as r:
                for u in range(RING):
                    transpose_rows(RING * r + (RING + u), u, r + 1)
                    if u % 2:
                        h = u // 2
                        eager(2 * r + (1 + h), (1 + h) % 2)

            def gather(c, lo, hi):
                acc = bank[c % 2]
                if lo == 0 and c >= 4:
                    pe.wait_ge(acc_copied, c - 1)
                if c == 2 and hi == NT:
                    pe.wait_ge(scale_step, 3 * NPAIR)
                for j in range(lo, hi):
                    mm = nc.tensor.matmul(acc[:, 0:2 * P], scaled[:, j, :], blocks[:, 2 * c:2 * c + 2, j, :],
                                          start=j == 0, stop=j == NT - 1)
                if hi == NT:
                    mm.then_inc(acc_done, 1)

            def back(c):
                pe.wait_ge(acc_copied, c + 1)
                if c:
                    pe.wait_ge(mix_step, 6 * c - 4)
                for t in range(2):
                    mm = nc.tensor.transpose(bank[2][:, t * P:(t + 1) * P], acc_sb[:, c % 2, t, :], ident[:])
                mm.then_inc(back_psum, 1)

            def turn_rows(c):
                pe.wait_ge(rows_ready, c + 1)
                if c:
                    pe.wait_ge(rowsT_ready, c)
                for t in range(2):
                    mm = nc.tensor.transpose(bank[3][:, t * P:(t + 1) * P], rows[:, c % 2, t, 0, 0:D], ident[:])
                mm.then_inc(rowsT_psum, 1)

            def logits(c):
                pe.wait_ge(rowsT_ready, c + 1)
                if c:
                    pe.wait_ge(pick_step, 6 * c - 3)
                for t in range(2):
                    o = bank[5][:, t * E:(t + 1) * E]
                    nc.tensor.matmul(o, xT2[:, c % 2, t, :], gate_sb[:], start=True, stop=False)
                    mm = nc.tensor.matmul(o, ones_row[:], gate_b_row[:], start=False, stop=True)
                mm.then_inc(logits_psum, 1)

            def ranks(c):
                pe.wait_ge(member_ready, c + 1)
                if c:
                    pe.wait_ge(members_ready, 2 * c)
                    pe.wait_ge(gate_step, 2 * c - 1)
                for t in range(2):
                    o = bank[6][:, t * E:(t + 1) * E]
                    nc.tensor.matmul(o, ones_row[:], region_row[:], start=True, stop=False)
                    nc.tensor.matmul(o, ones[:], members[:, c % 2, :], start=False, stop=False)
                    if t:
                        nc.tensor.matmul(o, ones[:], member[:, c % 2, 0, :], start=False, stop=False)
                    mm = nc.tensor.matmul(o, before[:], member[:, c % 2, t, :], start=False, stop=True)
                mm.then_inc(rank_psum, 1)

            pe.wait_ge(copied, NT * GROUPS)
            pe.wait_ge(consts, NCONST)
            gather(2, 0, 10)
            eager(NPAIR - 1, 1, stop=True)
            gather(2, 10, 11)
            back(0)
            gather(2, 11, NT)
            gather(3, 0, 1)
            turn_rows(0)
            gather(3, 1, 2)
            back(1)
            gather(3, 2, 3)
            logits(0)
            gather(3, 3, 7)
            back(2)
            ranks(0)
            gather(3, 7, 8)
            turn_rows(1)
            gather(3, 8, 10)
            logits(1)
            gather(3, 10, NT)
            ranks(1)
            turn_rows(2)
            gather(4, 0, 2)
            logits(2)
            gather(4, 2, 3)
            back(3)
            gather(4, 3, 6)
            ranks(2)
            gather(4, 6, 10)
            turn_rows(3)
            gather(4, 10, 12)
            logits(3)
            gather(4, 12, NT)
            for c in range(4, NPAIR - 1):
                gather(c + 1, 0, 1)
                back(c)
                ranks(c - 1)
                gather(c + 1, 1, 8)
                turn_rows(c)
                gather(c + 1, 8, 11)
                logits(c)
                gather(c + 1, 11, NT)
            back(NPAIR - 1)
            ranks(NPAIR - 2)
            turn_rows(NPAIR - 1)
            logits(NPAIR - 1)
            ranks(NPAIR - 1)

            pe.wait_ge(members_ready, 2 * NPAIR)
            nc.tensor.matmul(bank[4][0:NTP, 0:E], ones[:, 0:NTP], members[:, NPAIR % 2, :],
                             start=True, stop=True).then_inc(count_psum, 1)
            pe.wait_ge(tab_step, 14)
            for n in range(2):
                mm = nc.tensor.matmul(bank[7][0:1, n * NTP:(n + 1) * NTP], table_col[:, n:n + 1],
                                      ident[0:NTP, 0:NTP], start=True, stop=True)
            mm.then_inc(tab_psum, 1)

            pe.wait_ge(table_ready, 1)
            pe.wait_ge(w_loaded, 16 * 4)

            def step(s, u, q, stages, at):
                if 0 in stages:
                    pe.wait_ge(xg_loaded[u], 16 * (q + 1))
                    nc.tensor.transpose(bank[u % 2][:, 0:P], xg[:, u, 0:D], ident[:]).then_inc(xgT_psum, 1)
                if 1 in stages:
                    v = (u - 1) % 2
                    pe.wait_ge(xgT_ready, s)
                    nc.tensor.matmul(bank[2 + v][:], xgT[:, v, :], w_all[:, bass.ds(at(1), BANK)],
                                     start=True, stop=True).then_inc(h_psum, 1)
                if 2 in stages:
                    v = u % 2
                    pe.wait_ge(hid_ready, s - 1)
                    for c in range(HC):
                        mm = nc.tensor.transpose(bank[4 + v][:, c * P:(c + 1) * P], hid[:, v, c * P:(c + 1) * P],
                                                 ident[:])
                    mm.then_inc(hidT_psum, 1)
                if 3 in stages:
                    v = (u - 3) % 2
                    pe.wait_ge(hidT_ready, s - 2)
                    if 2 not in stages:
                        pe.wait_ge(y_ready, s - 4)
                    for c in range(HC):
                        mm = nc.tensor.matmul(bank[6 + v][:, 0:D], hidT[:, v, c * P:(c + 1) * P],
                                              w_all[:, bass.ds(at(3) + (BANK + c * D), D)], start=c == 0, stop=c == HC - 1)
                    mm.then_inc(y_psum, 1)

            steps(pe, step, lambda first, n: load_values(pe, first + NTP, n, (E - 1) * WROW))

        @block.scalar
        def _(act):
            act.dma_start(w_nat[:], w_gnn).then_inc(par_loaded, 16)
            act.dma_start(b_row[:], b_gnn.rearrange("(a n) -> a n", a=1)).then_inc(par_loaded, 16)
            act.dma_start(gate_sb[:], gate_w).then_inc(par_loaded, 16)
            act.dma_start(gate_b_row[:], gate_b.rearrange("(a n) -> a n", a=1)).then_inc(par_loaded, 16)
            act.wait_ge(wb_psum, 1)
            nc.scalar.copy(w_t[:], bank[4][:, 0:P]).then_inc(wb_ready, 1)
            nc.scalar.copy(b_all[:], bank[4][:, P:P + D]).then_inc(wb_ready, 1)

            def copy_xn(g):
                act.wait_ge(xnt_psum, g + 1)
                if g >= 2:
                    act.wait_ge(sup_psum, g - 1)
                nc.scalar.copy(xn_t[:, g % 2, :], bank[5 + g % 2][:]).then_inc(xnt_ready, 1)

            def copy_rows(k):
                for g in range(GROUPS):
                    act.wait_ge(transposed, k * GROUPS + g + 1)
                    nc.scalar.copy(adjT[:, bass.ds(k * N + g * BANK, BANK)], bank[g][:]).then_inc(copied, 1)

            copy_xn(0)
            for k in range(RING):
                copy_rows(k)
                if k + 1 < NXG:
                    copy_xn(k + 1)
            with act.Fori(0, NT - RING) as k:
                copy_rows(RING + k)

            def copy_acc(c):
                if c >= 2:
                    act.wait_ge(back_psum, c - 1)
                if c < 2:
                    act.wait_ge(eager_done, 1)
                    src = bank[4][:, c * 2 * P:(c + 1) * 2 * P]
                else:
                    act.wait_ge(acc_done, c - 1)
                    src = bank[c % 2][:, 0:2 * P]
                nc.scalar.copy(acc_sb[:, c % 2].rearrange("p t n -> p (t n)"), src).then_inc(acc_copied, 1)

            def route(c):
                if c >= 2:
                    act.wait_ge(rows_sent[c % 2], 16 * 2 * TOPK * (c // 2))
                nc.scalar.copy(rows[:, c % 2, :, :, D + 1].bitcast(I32), dest[:, 2 * c:2 * c + 2, :]).then_inc(dest_ready, 1)
                act.wait_ge(rowsT_psum, c + 1)
                nc.scalar.copy(xT2[:, c % 2].rearrange("p t n -> p (t n)"), bank[3][:, 0:2 * P]).then_inc(rowsT_ready, 1)
                act.wait_ge(gap_ready, c + 1)
                nc.scalar.activation(e_gap[:], gap[:], ACT.Exp).then_inc(e_ready, 1)

            act.wait_ge(consts, NCONST)
            copy_acc(0)
            copy_acc(1)
            route(0)
            copy_acc(2)
            route(1)
            for c in range(2, NPAIR):
                route(c)
                if c + 1 < NPAIR:
                    copy_acc(c + 1)

            def step(s, u, q, stages, at):
                if 1 in stages:
                    v = (u - 1) % 2
                    act.wait_ge(h_psum, s)
                    nc.scalar.activation(sil[:, v, :], bank[2 + v][:, 0:HID], ACT.Silu).then_inc(sil_ready, 1)
                if 2 in stages:
                    v = u % 2
                    act.wait_ge(hidT_psum, s - 1)
                    nc.scalar.copy(hidT[:, v, :], bank[4 + v][:, 0:HID]).then_inc(hidT_ready, 1)

            steps(act, step)

        @block.vector
        def _(dve):
            def x_moments(g):
                at = 2 * XG * g
                dve.wait_ge(x_loaded[g], 16)
                for n in range(XG):
                    nc.vector.bn_stats(x_stats[:, g * XG + n, :], x_mid[:, g * XG + n, :]).then_inc(x_stat, 1)
                for n in range(XG):
                    dve.wait_ge(x_stat, at + n + 1)
                    nc.vector.bn_aggr(x_mv[:, g * XG + n, :], x_stats[:, g * XG + n, :]).then_inc(x_stat, 1)
                dve.wait_ge(x_stat, at + 2 * XG)
                part = slice(g * XG, (g + 1) * XG)
                nc.vector.tensor_scalar(x_var[:, part], x_mv[:, part, 1], EPS, None, ALU.add).then_inc(x_var_ready, 1)

            def normalise_x(g):
                dve.wait_ge(x_rstd_ready, g + 1)
                for i in range(g * XG, (g + 1) * XG):
                    nc.vector.tensor_scalar(support[:, i, :], x_mid[:, i, :], x_mv[:, i, 0:1], x_rstd[:, i:i + 1],
                                            ALU.subtract, ALU.mult).then_inc(xn_ready, 1)

            def add_b(g):
                dve.wait_ge(sup_psum, g + 1)
                dve.wait_ge(wb_ready, 2)
                nc.vector.tensor_tensor(support[:, g * XG:(g + 1) * XG, :],
                                        bank[7][:].rearrange("p (i d) -> p i d", d=D),
                                        b_all[:].unsqueeze(1).to_broadcast([P, XG, D]), ALU.add).then_inc(sup_ready, 1)

            def sum_rows(k, u, first=False):
                if first:
                    dve.wait_ge(a_loaded[0], 16)
                else:
                    dve.wait_ge(fold_done, k)
                nc.vector.tensor_reduce(row_sum[:, bass.ds(k, 1)], a_rows[:, 0, :] if first else folded[:, u % 2, :],
                                        AX_X, ALU.add).then_inc(row_step, 1)

            def take_degree(c):
                pair = bass.ds(2 * c, 2)
                dve.wait_ge(row_step, 4 * c + 2)
                nc.vector.tensor_scalar(no_degree[:, pair], row_sum[:, pair], -1.0, None, ALU.is_equal).then_inc(row_step, 1)
                dve.wait_ge(row_step, 4 * c + 3)
                nc.vector.scalar_tensor_tensor(out=degree[:, pair], in0=row_sum[:, pair], scalar=1.0,
                                               in1=no_degree[:, pair], op0=ALU.add, op1=ALU.add).then_inc(row_step, 1)

            def scale_rows(c, h, first=False):
                pair = bass.ds(2 * c, 2)
                dve.wait_ge(root_ready, c + 1)
                nc.vector.tensor_tensor(dinv[:, pair], root[:, pair], no_degree[:, pair], ALU.subtract).then_inc(scale_step, 1)
                dve.wait_ge(scale_step, 3 * c + 1)
                if not first:
                    dve.wait_ge(transposed, 2 * c * GROUPS + 1)
                now = scaled_now[:, 2 * h:2 * h + 2, :]
                nc.vector.tensor_tensor(now, support[:, pair, :],
                                        dinv[:, pair].unsqueeze(2).to_broadcast([P, 2, D]), ALU.mult).then_inc(scale_step, 1)
                dve.wait_ge(scale_step, 3 * c + 2)
                nc.vector.tensor_copy(scaled[:, pair, :], now)
                for t in range(2):
                    row = x_mid[:, bass.ds(2 * c + t, 1), :].rearrange("p a d -> p (a d)")
                    v = nc.vector.scalar_tensor_tensor(out=row, in0=now[:, t, :], scalar=dinv[:, bass.ds(2 * c + t, 1)],
                                                       in1=row, op0=ALU.mult, op1=ALU.add)
                v.then_inc(scale_step, 1)

            x_moments(0)
            x_moments(1)
            normalise_x(0)
            x_moments(2)
            normalise_x(1)
            x_moments(3)
            sum_rows(0, 0, first=True)
            normalise_x(2)
            add_b(0)
            sum_rows(1, 1)
            take_degree(0)
            normalise_x(3)
            add_b(1)
            sum_rows(2, 2)
            scale_rows(0, 0, first=True)
            sum_rows(3, 3)
            take_degree(1)
            add_b(2)
            add_b(3)
            with dve.Fori(0, NT // RING - 1) as r:
                for h in range(2):
                    k, c = RING * r + (RING + 2 * h), 2 * r + (2 + h)
                    sum_rows(k, 0)
                    scale_rows(2 * r + (1 + h), (1 + h) % 2)
                    sum_rows(RING * r + (RING + 2 * h + 1), 1)
                    take_degree(c)
            scale_rows(NPAIR - 1, 1)

            def mix(c):
                dve.wait_ge(back_psum, c + 1)
                for t in range(2):
                    i = 2 * c + t
                    nc.vector.scalar_tensor_tensor(out=x_mid[:, i, :], in0=bank[2][:, t * P:(t + 1) * P],
                                                   scalar=dinv[:, i:i + 1], in1=x_mid[:, i, :],
                                                   op0=ALU.mult, op1=ALU.add).then_inc(mix_step, 1)
                for t in range(2):
                    dve.wait_ge(mix_step, 6 * c + 1 + t)
                    nc.vector.bn_stats(stats[:, t, :], x_mid[:, 2 * c + t, :]).then_inc(mix_step, 1)
                for t in range(2):
                    dve.wait_ge(mix_step, 6 * c + 3 + t)
                    nc.vector.bn_aggr(mv[:, t, :], stats[:, t, :]).then_inc(mix_step, 1)
                dve.wait_ge(mix_step, 6 * c + 6)
                nc.vector.tensor_scalar(var[:], mv[:, :, 1], EPS, None, ALU.add).then_inc(var_ready, 1)

            def fill_rows(c):
                dve.wait_ge(rstd_ready, c + 1)
                if c >= 2:
                    dve.wait_ge(rows_sent[c % 2], 16 * 2 * TOPK * (c // 2))
                for k in range(TOPK):
                    for t in range(2):
                        v = nc.vector.tensor_scalar(rows[:, c % 2, t, k, 0:D], x_mid[:, 2 * c + t, :], mv[:, t, 0:1],
                                                    rstd[:, t:t + 1], ALU.subtract, ALU.mult)
                    if k == 0:
                        v.then_inc(rows_ready, 1)

            def choose(c):
                at = 6 * c
                dve.wait_ge(logits_psum, c + 1)
                for t in range(2):
                    nc.vector.max(best[:, t, :], bank[5][:, t * E:(t + 1) * E]).then_inc(pick_step, 1)
                dve.wait_ge(pick_step, at + 2)
                nc.vector.tensor_tensor(gap[:], best[:, :, 1], best[:, :, 0], ALU.subtract).then_inc(gap_ready, 1)
                for t in range(2):
                    v = nc.vector.max_index(best_at[:, t, :], best[:, t, :], bank[5][:, t * E:(t + 1) * E])
                v.then_inc(pick_step, 1)
                dve.wait_ge(pick_step, at + 3)
                for k in range(TOPK):
                    v = nc.vector.tensor_tensor(chosen[:, k], iota_e[:].unsqueeze(1).to_broadcast([P, 2, E]),
                                                best_at[:, :, k:k + 1].to_broadcast([P, 2, E]), ALU.is_equal)
                v.then_inc(pick_step, 1)
                dve.wait_ge(pick_step, at + 4)
                nc.vector.tensor_tensor(member[:, c % 2], chosen[:, 0], chosen[:, 1], ALU.add).then_inc(member_ready, 1)
                dve.wait_ge(member_ready, c + 1)
                nc.vector.tensor_tensor(members[:, 2, :], members[:, c % 2, :], member[:, c % 2, 0, :],
                                        ALU.add).then_inc(members_ready, 1)
                dve.wait_ge(members_ready, 2 * c + 1)
                nc.vector.tensor_tensor(members[:, (c + 1) % 2, :], members[:, 2, :], member[:, c % 2, 1, :],
                                        ALU.add).then_inc(members_ready, 1)
                dve.wait_ge(e_ready, c + 1)
                nc.vector.tensor_scalar(e_sum[:], e_gap[:], 1.0, None, ALU.add).then_inc(pick_step, 1)
                dve.wait_ge(pick_step, at + 5)
                nc.vector.reciprocal(rows[:, c % 2, :, 0, D], e_sum[:]).then_inc(pick_step, 1)

            def place(c):
                dve.wait_ge(pick_step, 6 * c + 6)
                nc.vector.tensor_tensor(rows[:, c % 2, :, 1, D], e_gap[:], rows[:, c % 2, :, 0, D], ALU.mult)
                dve.wait_ge(rank_psum, c + 1)
                for k in range(TOPK):
                    v = nc.vector.tensor_tensor(picked[:, k], chosen[:, k],
                                                bank[6][:, 0:2 * E].rearrange("p (t e) -> p t e", t=2), ALU.mult)
                v.then_inc(gate_step, 1)
                dve.wait_ge(gate_step, 2 * c + 1)
                nc.vector.tensor_reduce(slot_f[:], picked[:], AX_X, ALU.add).then_inc(gate_step, 1)
                dve.wait_ge(gate_step, 2 * c + 2)
                nc.vector.tensor_copy(slot[:, c % 2], slot_f[:]).then_inc(slot_ready, 1)

            dve.wait_ge(consts, NCONST)
            dve.wait_ge(scale_step, 3 * NPAIR)
            for c in range(NPAIR):
                mix(c)
                if c:
                    place(c - 1)
                fill_rows(c)
                choose(c)
            place(NPAIR - 1)

            chain = [0]

            def link(v):
                chain[0] += 1
                v.then_inc(tab_step, 1)
                dve.wait_ge(tab_step, chain[0])

            dve.wait_ge(count_psum, 1)
            link(nc.vector.tensor_copy(cnt[:], bank[4][0:NTP, 0:E]))
            link(nc.vector.tensor_scalar(cnt_up[:], cnt[:], float(P - 1), None, ALU.add))
            link(nc.vector.tensor_scalar(tiles_i[:], cnt_up[:], P.bit_length() - 1, None, ALU.arith_shift_right))
            link(nc.vector.tensor_copy(tiles_f[:], tiles_i[:]))
            link(nc.vector.tensor_tensor_scan(upto[:], tiles_f[:], zeros_e[:], 0.0, ALU.add, ALU.add))
            link(nc.vector.tensor_tensor(prior[:], upto[:], tiles_f[:], ALU.subtract))
            link(nc.vector.scalar_tensor_tensor(out=end_row[:], in0=prior[:], scalar=float(P), in1=cnt[:],
                                                op0=ALU.mult, op1=ALU.add))
            link(nc.vector.tensor_tensor(end_row[:], end_row[:], region_col[:], ALU.add))
            link(nc.vector.tensor_scalar(passed[:], upto[:], tile_no[:], 0.0, ALU.is_le, ALU.add, accum_out=n_passed[:]))
            link(nc.vector.scalar_tensor_tensor(out=is_own[:], in0=prior[:], scalar=tile_no[:], in1=passed[:],
                                                op0=ALU.is_le, op1=ALU.subtract))
            link(nc.vector.scalar_tensor_tensor(out=end_row[:], in0=is_own[:], scalar=1.0, in1=end_row[:],
                                                op0=ALU.mult, op1=ALU.mult, accum_out=start_sum[:]))
            link(nc.vector.tensor_scalar(live[:], n_passed[:], float(E), None, ALU.is_lt))
            link(nc.vector.tensor_scalar(start_sum[:], start_sum[:], tile_row[:], float(-NULL_ROW), ALU.subtract, ALU.add))
            nc.vector.tensor_scalar(table_col[:, 0:1], start_sum[:], live[:], float(NULL_ROW), ALU.mult, ALU.add)
            nc.vector.tensor_scalar(table_col[:, 1:2], n_passed[:], float(E - 1), float(WROW), ALU.min,
                                    ALU.mult).then_inc(tab_step, 1)
            dve.wait_ge(tab_psum, 1)
            nc.vector.tensor_copy(table[:], bank[7][0:1, 0:2 * NTP]).then_inc(table_ready, 1)

            def step(s, u, q, stages, at):
                if 0 in stages:
                    dve.wait_ge(xgT_psum, s + 1)
                    nc.vector.tensor_copy(xgT[:, u % 2, :], bank[u % 2][:, 0:P]).then_inc(xgT_ready, 1)
                    if not isinstance(s, int) or s >= RING:
                        dve.wait_ge(y_ready, s - LAG)
                    nc.vector.tensor_copy(meta[:, u, :], xg[:, u, D:ROW]).then_inc(meta_ready, 1)
                if 1 in stages:
                    v = (u - 1) % 2
                    dve.wait_ge(sil_ready, s)
                    nc.vector.tensor_tensor(hid[:, v, :], sil[:, v, :], bank[2 + v][:, HID:BANK],
                                            ALU.mult).then_inc(hid_ready, 1)
                if 3 in stages:
                    v, w = (u - 3) % 2, (u - 3) % RING
                    dve.wait_ge(y_psum, s - 2)
                    if not isinstance(s, int) or s - LAG >= RING:
                        dve.wait_ge(y_sent[w], 16 * (q_of(s, q, u)))
                    dve.wait_ge(meta_ready, s - 2)
                    nc.vector.tensor_copy(y_dest[:, w, :], meta[:, w, 1:2])
                    nc.vector.tensor_scalar(y_out[:, w, :], bank[6 + v][:, 0:D], meta[:, w, 0:1], None,
                                            ALU.mult).then_inc(y_ready, 1)

            def q_of(s, q, u):
                return q - (1 if u < LAG else 0)

            steps(dve, step)

            per = NT // RING
            for q in range(RING):
                part = slice(q * per, (q + 1) * per)
                dve.wait_ge(z_loaded[q], 16)
                nc.vector.tensor_tensor(z_buf[:, part, 0, :], z_buf[:, part, 0, :], z_buf[:, part, 1, :],
                                        ALU.add).then_inc(z_sum, 1)
                dve.wait_ge(z_sum, q + 1)
                nc.vector.tensor_tensor(x_mid[:, part, :], x_mid[:, part, :], z_buf[:, part, 0, :],
                                        ALU.add).then_inc(out_ready, 1)


_INS = ["x", "adj", "L0_gnn_W", "L0_gnn_b", "L0_ffn_gate_w", "L0_ffn_gate_b", "L0_ffn_w1", "L0_ffn_w2", "L0_ffn_w3"]


def kernel(**inputs):
    import concourse.bacc as bacc
    from concourse.bass_utils import run_bass_kernel_spmd

    nc = bacc.Bacc("TRN2", target_bir_lowering=False, num_devices=1)
    arrays, args = {}, []
    for name in _INS:
        a = np.ascontiguousarray(inputs[name])
        arrays[f"in_{name}"] = a
        args.append(nc.dram_tensor(f"in_{name}", a.shape, mybir.dt.from_np(a.dtype), kind="ExternalInput").ap())
    out = nc.dram_tensor("out", inputs["x"].shape, F32, kind="ExternalOutput").ap()
    graph_moe(nc, *args, out)
    r = run_bass_kernel_spmd(nc, [arrays], core_ids=[0])
    return r.results[0]["out"]
```

```python
from contextlib import ExitStack
from itertools import count, islice

import numpy as np

import concourse.bass as bass
from concourse import mybir

F32 = mybir.dt.float32
F32R = mybir.dt.float32r
BF16 = mybir.dt.bfloat16
I32 = mybir.dt.int32
U32 = mybir.dt.uint32
ALU = mybir.AluOpType
ACT = mybir.ActivationFunctionType
AX_X = mybir.AxisListType.X

P = 128
BANK = 512
EPS = 1e-5


def graph_moe(nc, x, adj, w_gnn, b_gnn, gate_w, gate_b, w1, w2, w3, out):
    N, D = x.shape
    E, _, HID = w1.shape
    NT = N // P
    TOPK = 2
    RING = 4
    EAGER = BANK // P
    NPAIR = NT // 2
    XG = BANK // D
    NXG = NT // XG
    BLOCKS = BANK // P
    GROUPS = NT // BLOCKS
    HALF = N // 2
    HC = HID // P
    REGION = P + N
    NULL_ROW = E * REGION
    SLOTS = TOPK * N
    NTILE = SLOTS // P + E - 1
    ROW = D + 2
    NTP = NTILE + 1
    GROUP = [(i, 2) for i in range(0, NT - 2, 2)] + [(NT - 2, 1), (NT - 1, 1)]
    NG = len(GROUP)
    cuts = [0, NT // 4, NT // 2, 3 * NT // 4, 7 * NT // 8, NT]
    PART = [slice(lo, hi) for lo, hi in zip(cuts, cuts[1:])]
    NEG = EAGER // 2
    assert REGION % P == 0 and (E * REGION) // P <= 272 and ((E - 1) * REGION) // P + 1 <= 256
    assert D == P and HC == 2 and 2 * HID == BANK and NT % RING == 0 and EAGER == RING

    with ExitStack() as ctx:
        def sb(name, shape, dtype=F32):
            return ctx.enter_context(nc.sbuf_tensor(name, shape, dtype))

        def sem(name):
            return ctx.enter_context(nc.semaphore(name))

        x_sorted = nc.dram_tensor("x_sorted", [NULL_ROW + P, ROW], F32, kind="Internal").ap()
        y_tokens = nc.dram_tensor("y_tokens", [SLOTS, D], F32, kind="Internal").ap()

        a_rows = sb("a_rows", [P, RING, N])
        folded = sb("folded", [P, 2, HALF])
        x_mid = sb("x_mid", [P, NT, D])
        support = sb("support", [P, NT, D])
        scaled = sb("scaled", [P, NT, D])
        xn_t = scaled[:, NT - 2 * XG:NT, :].rearrange("p (u i) d -> p u (i d)", u=2)
        scaled_now = sb("scaled_now", [P, RING, D])
        w_nat = sb("w_nat", [P, D])
        w_t = sb("w_t", [P, D])
        b_row = sb("b_row", [1, D])
        gate_sb = sb("gate_sb", [P, E])
        gate_b_row = sb("gate_b_row", [1, E])
        gate_b3 = sb("gate_b3", [1, 3, 2, E], BF16)
        gate_b_rest = sb("gate_b_rest", [1, 2, 2, E])
        ident = sb("ident", [P, P])
        ones_row = sb("ones_row", [1, P])
        before = sb("before", [P, P], BF16)
        ones = sb("ones", [P, P], BF16)
        iota_e = sb("iota_e", [P, E])
        region_row = sb("region_row", [1, 2, E])
        region_bf = sb("region_bf", [1, 2, E], BF16)
        region_col = sb("region_col", [NTP, E])
        tile_no = sb("tile_no", [NTP, 1])
        tile_row = sb("tile_row", [NTP, 1])
        dest = sb("dest", [P, NT, TOPK], I32)
        minus_half = sb("minus_half", [P, NT])
        pad = sb("pad", [P, ROW])
        xgT = sb("xgT", [P, 2, 2, P], F32R)
        b_all = sb("b_all", [P, D])
        x_stats = sb("x_stats", [P, NT, 6])
        x_mv = sb("x_mv", [P, NT, 2])
        x_var = sb("x_var", [P, NT])
        x_rstd = sb("x_rstd", [P, NT])
        row_sum = sb("row_sum", [P, NT])
        no_degree = sb("no_degree", [P, NT])
        degree = sb("degree", [P, NT])
        root = sb("root", [P, NT])
        dinv = sb("dinv", [P, NT])
        stats = sb("stats", [P, 2, 6])
        mv = sb("mv", [P, 2, 2, 2])
        var = sb("var", [P, 2])
        rstd = sb("rstd", [P, 2, 2])
        best = sb("best", [P, 2, 8])
        best_at = sb("best_at", [P, 2, 8], U32)
        gap = sb("gap", [P, 2])
        e_gap = sb("e_gap", [P, 2])
        e_sum = sb("e_sum", [P, 2])
        chosen = sb("chosen", [P, TOPK, 2, E])
        member = sb("member", [P, 2, 2, E], BF16)
        members = sb("members", [P, 3, E], BF16)
        picked = sb("picked", [P, TOPK, 2, E])
        slot = sb("slot", [P, RING, TOPK, 2], U32)
        cnt_up = sb("cnt_up", [NTP, E], I32)
        tiles_i = sb("tiles_i", [NTP, E], I32)
        tiles_f = sb("tiles_f", [NTP, E])
        zeros_e = sb("zeros_e", [NTP, E])
        upto = sb("upto", [NTP, E])
        prior = sb("prior", [NTP, E])
        end_row = sb("end_row", [NTP, E])
        passed = sb("passed", [NTP, E])
        is_own = sb("is_own", [NTP, E])
        n_passed = sb("n_passed", [NTP, 1])
        live = sb("live", [NTP, 1])
        start_sum = sb("start_sum", [NTP, 1])
        start_row = sb("start_row", [NTP, 1])
        first_row = sb("first_row", [NTP, E])
        picked_row = sb("picked_row", [NTP, E])
        table_col = sb("table_col", [NTP, 2])
        table = sb("table", [1, 2 * NTP], I32)
        meta = sb("meta", [P, RING, 2])
        y_dest = sb("y_dest", [P, RING, 1])

        LOW, HIGH, W3 = 0, BANK, 2 * BANK
        WROW = 2 * BANK + HID
        def at_same_place(name, shape, dtype=F32):
            with nc.sbuf_tensor(name, shape, dtype) as tensor:
                return tensor

        w_raw = at_same_place("w_raw", [P, E * WROW])
        w_parts = at_same_place("w_parts", [P, E * WROW], F32R)
        adjT = sb("adjT", [P, NT * N])
        z_at = 10 * N
        z_buf = adjT[:, z_at:z_at + NT * TOPK * D].rearrange("p (i k d) -> p i k d", k=TOPK, d=D)
        W_STAGE, e = [], 0
        for done in (EAGER, EAGER + 2, EAGER + 4, EAGER + 6):
            upto_e = min(E, done * N // WROW)
            W_STAGE.append((e, upto_e))
            e = upto_e
        assert e == E and z_at >= E * WROW

        late = a_rows[:].rearrange("p u n -> p (u n)")
        used = 0

        def over(shape, pattern=None, **sizes):
            nonlocal used
            n = int(np.prod(shape))
            part = late[:, used:used + n]
            used += n
            return part.rearrange(pattern, **sizes) if pattern else part

        acc_sb = over([2, 2, P], "p (c t n) -> p c t n", c=2, t=2)
        rows = over([RING, 2, TOPK, ROW], "p (c t k n) -> p c t k n", c=RING, t=2, k=TOPK)
        xT2 = over([2, 2, P], "p (c t n) -> p c t n", c=2, t=2)
        xg = over([RING, ROW], "p (u n) -> p u n", u=RING)
        sil = over([2, HID], "p (u n) -> p u n", u=2)
        hid = over([2, HID], "p (u n) -> p u n", u=2)
        hidT = over([2, HID], "p (u n) -> p u n", u=2)
        y_out = over([RING, D], "p (u n) -> p u n", u=RING)
        assert used <= RING * N

        bank = [ctx.enter_context(nc.psum_tensor(f"bank{i}", [P, BANK], F32)) for i in range(8)]

        consts = sem("consts")
        fill = sem("fill")
        x_loaded = [sem(f"x_loaded{i}") for i in range(NXG)]
        par_loaded = sem("par_loaded")
        a_loaded = [sem(f"a_loaded{i}") for i in range(RING)]
        x_stat = sem("x_stat")
        x_var_ready = sem("x_var_ready")
        x_rstd_ready = sem("x_rstd_ready")
        xn_ready = sem("xn_ready")
        wb_psum = sem("wb_psum")
        wb_ready = sem("wb_ready")
        xnt_psum = sem("xnt_psum")
        xnt_ready = sem("xnt_ready")
        sup_psum = sem("sup_psum")
        sup_ready = sem("sup_ready")
        transposed = sem("transposed")
        copied = sem("copied")
        fold_done = sem("fold_done")
        row_step = sem("row_step")
        root_ready = sem("root_ready")
        scale_step = sem("scale_step")
        eager_done = sem("eager_done")
        acc_done = sem("acc_done")
        acc_copied = sem("acc_copied")
        back_psum = sem("back_psum")
        mix_step = sem("mix_step")
        var_ready = sem("var_ready")
        rstd_ready = sem("rstd_ready")
        rows_ready = sem("rows_ready")
        dest_ready = sem("dest_ready")
        rowsT_psum = sem("rowsT_psum")
        rowsT_ready = sem("rowsT_ready")
        logits_psum = sem("logits_psum")
        gap_ready = sem("gap_ready")
        e_ready = sem("e_ready")
        pick_step = sem("pick_step")
        member_ready = sem("member_ready")
        members_ready = sem("members_ready")
        rank_psum = sem("rank_psum")
        gate_step = sem("gate_step")
        slot_ready = sem("slot_ready")
        rows_sent = [sem(f"rows_sent{i}") for i in range(RING)]
        bias_step = sem("bias_step")
        pads_sent = sem("pads_sent")
        count_psum = sem("count_psum")
        tab_step = sem("tab_step")
        tab_psum = sem("tab_psum")
        table_ready = sem("table_ready")
        w_loaded = [sem(f"w_loaded{i}") for i in range(len(W_STAGE))]
        high_ready = sem("high_ready")
        low_dve = sem("low_dve")
        low_pool = sem("low_pool")
        xgT_high = sem("xgT_high")
        xg_loaded = [sem(f"xg_loaded{i}") for i in range(RING)]
        xgT_psum = sem("xgT_psum")
        xgT_ready = sem("xgT_ready")
        meta_ready = sem("meta_ready")
        h_psum = sem("h_psum")
        sil_ready = sem("sil_ready")
        hid_ready = sem("hid_ready")
        hidT_psum = sem("hidT_psum")
        hidT_ready = sem("hidT_ready")
        y_psum = sem("y_psum")
        y_ready = sem("y_ready")
        y_sent = [sem(f"y_sent{i}") for i in range(RING)]
        z_loaded = [sem(f"z_loaded{i}") for i in range(len(PART))]
        z_sum = sem("z_sum")
        out_ready = sem("out_ready")
        out_sent = sem("out_sent")

        NCONST = 15

        def sent(g):
            return 16 * TOPK * sum(GROUP[i][1] for i in range(g % RING, g + 1, RING))

        serial = count()

        LAG = 3
        head = LAG + RING
        UNROLL = 2 * RING
        assert (NTILE - LAG - RING) % UNROLL == 0

        def load_values(eng, first, n, most):
            regs = [eng.alloc_register(f"{eng.engine}_entry{i}_{next(serial)}") for i in range(n)]
            eng.load(regs, table[0:1, bass.ds(first, n)])
            return [eng.snap(reg, min_val=0, max_val=most) for reg in regs]

        def steps(eng, step, lags=(0, 1, 2, 3), load_weight_columns=None):
            load = load_weight_columns or (lambda first, n: None)
            last = lags[-1]

            def active(s):
                return [i for i, lag in enumerate(lags) if 0 <= s - lag < NTILE]

            v = load(0, head - 1)
            for s in range(head):
                step(s, s % RING, s // RING, active(s), lambda n: v[s - n])
            first = (head - last) // 4 * 4
            with eng.Fori(0, (NTILE - head) // UNROLL) as r:
                v = load(UNROLL * r + first, head + UNROLL - 1 - first)
                for i in range(UNROLL):
                    s = head + i
                    step(UNROLL * r + s, s % RING, UNROLL // RING * r + s // RING, range(len(lags)),
                         lambda n: v[s - n - first])
            first = (NTILE - last) // 4 * 4
            v = load(first, NTILE - first)
            for s in range(NTILE, NTILE + last):
                step(s, s % RING, s // RING, active(s), lambda n: v[s - n - first])

        def acc_bank(g):
            return bank[7] if g == NEG else bank[g % 2]

        POOL_LOW = (0, 1, 2, E - 3, E - 2, E - 1)
        DVE_LOW = [e for e in range(E) if e not in POOL_LOW]

        def take_low(eng, tensor_tensor, e, done):
            eng.wait_ge(high_ready, e + 1)
            low = slice(e * WROW + LOW, e * WROW + LOW + BANK)
            high = slice(e * WROW + HIGH, e * WROW + HIGH + BANK)
            tensor_tensor(w_parts[:, low], w_raw[:, low], w_parts[:, high].bitcast(F32), ALU.subtract).then_inc(done, 1)

        block = ctx.enter_context(nc.Block())

        @block.sync
        def _(sp):
            x_v = x.rearrange("(i p) d -> p i d", p=P)
            for g in range(NXG):
                part = slice(g * XG, (g + 1) * XG)
                sp.dma_start(x_mid[:, part], x_v[:, part]).then_inc(x_loaded[g], 16)

            def load_rows(k, u):
                sp.dma_start(a_rows[:, u, :], adj[bass.ds(k * P, P), :]).then_inc(a_loaded[u], 16)

            for u in range(RING):
                load_rows(u, u)
            with sp.Fori(0, NT // RING - 1) as r:
                for u in range(RING):
                    sp.wait_ge(transposed, (RING * r + u + 1) * GROUPS)
                    if u:
                        sp.wait_ge(fold_done, RING * r + u)
                    else:
                        sp.wait_ge(row_step, 2 * RING * r + 1)
                    load_rows(RING * r + u + RING, u)
            sp.wait_ge(consts, NCONST)
            for e in range(E + 1):
                sp.dma_start(x_sorted[e * REGION:e * REGION + P, :], pad[:]).then_inc(pads_sent, 16)
            w_v = w_raw[:].rearrange("p (e n) -> p e n", e=E)
            for i, (lo, hi) in enumerate(W_STAGE):
                if i == 0:
                    sp.wait_ge(eager_done, 1)
                else:
                    sp.wait_ge(acc_done, i)
                sp.dma_start(w_v[:, lo:hi, LOW:LOW + HID], w1[lo:hi].rearrange("e d h -> d e h")).then_inc(w_loaded[i], 16)
                sp.dma_start(w_v[:, lo:hi, LOW + HID:LOW + BANK], w2[lo:hi].rearrange("e d h -> d e h")).then_inc(w_loaded[i], 16)
                for c in range(HC):
                    sp.dma_start(w_v[:, lo:hi, W3 + c * D:W3 + (c + 1) * D],
                                 w3[lo:hi, c * P:(c + 1) * P, :].rearrange("e h d -> h e d")).then_inc(w_loaded[i], 16)

            sp.wait_ge(table_ready, 1)
            first = load_values(sp, 0, RING, NULL_ROW)
            sp.wait_ge(pads_sent, 16 * (E + 1))
            for g in range(NG - RING, NG):
                sp.wait_ge(rows_sent[g % RING], sent(g))

            def load_tile(first, u):
                sp.dma_start(xg[:, u, :], x_sorted[bass.ds(first, P), :]).then_inc(xg_loaded[u], 16)

            for t in range(RING):
                load_tile(first[t], t)
            rounds = NTILE // RING
            with sp.Fori(0, rounds - 1) as r:
                first = load_values(sp, RING * r + RING, RING, NULL_ROW)
                for u in range(RING):
                    sp.wait_ge(meta_ready, RING * r + u + 1)
                    load_tile(first[u], u)
            first = load_values(sp, RING * rounds, NTILE - RING * rounds, NULL_ROW)
            for t in range(RING * rounds, NTILE):
                sp.wait_ge(meta_ready, t - RING + 1)
                load_tile(first[t % RING], t % RING)

            for u in range(RING):
                sp.wait_ge(y_sent[u], 16 * len(range(u, NTILE, RING)))
            z_dram = y_tokens.rearrange("(i p k) d -> p i (k d)", p=P, k=TOPK)
            for q, part in enumerate(PART):
                sp.dma_start(z_buf[:, part].rearrange("p i k d -> p i (k d)"), z_dram[:, part]).then_inc(z_loaded[q], 16)
            out_v = out.rearrange("(i p) d -> p i d", p=P)
            for q, part in enumerate(PART):
                sp.wait_ge(out_ready, q + 1)
                sp.dma_start(out_v[:, part], x_mid[:, part]).then_inc(out_sent, 16)
            sp.wait_ge(out_sent, 16 * len(PART))

        @block.gpsimd
        def _(pool):
            nc.gpsimd.memset(ident[:], 0.0).then_inc(fill, 1)
            nc.gpsimd.memset(before[:], 1.0).then_inc(fill, 1)
            nc.gpsimd.memset(pad[:], 0.0).then_inc(fill, 1)
            pool.wait_ge(fill, 3)
            nc.gpsimd.affine_select(out=ident[:], in_=ident[:], compare_op=ALU.not_equal, fill=1.0, base=0,
                                    pattern=[[-1, P]], channel_multiplier=1).then_inc(consts, 1)
            nc.gpsimd.memset(minus_half[:], -0.5).then_inc(consts, 1)
            nc.gpsimd.memset(ones_row[:], 1.0).then_inc(consts, 1)
            nc.gpsimd.affine_select(out=before[:], in_=before[:], compare_op=ALU.is_gt, fill=0.0, base=0,
                                    pattern=[[1, P]], channel_multiplier=-1).then_inc(consts, 1)
            nc.gpsimd.memset(ones[:], 1.0).then_inc(consts, 1)
            nc.gpsimd.memset(members[:], 0.0).then_inc(consts, 1)
            nc.gpsimd.memset(zeros_e[:], 0.0).then_inc(consts, 1)
            exact = dict(allow_small_or_imprecise_dtypes=True)
            nc.gpsimd.iota(iota_e[:], pattern=[[1, E]], base=0, channel_multiplier=0, **exact).then_inc(consts, 1)
            nc.gpsimd.iota(region_row[:], pattern=[[0, 2], [REGION, E]], base=P, channel_multiplier=0, **exact).then_inc(consts, 1)
            nc.gpsimd.iota(region_col[:], pattern=[[REGION, E]], base=0, channel_multiplier=0, **exact).then_inc(consts, 1)
            nc.gpsimd.iota(tile_no[:], pattern=[[0, 1]], base=0, channel_multiplier=1, **exact).then_inc(consts, 1)
            nc.gpsimd.iota(tile_row[:], pattern=[[0, 1]], base=0, channel_multiplier=P, **exact).then_inc(consts, 1)
            nc.gpsimd.iota(dest[:], pattern=[[TOPK * P, NT], [1, TOPK]], base=0, channel_multiplier=TOPK).then_inc(consts, 1)
            nc.gpsimd.iota(pad[:, D + 1:ROW].bitcast(I32), pattern=[[0, 1]], base=SLOTS, channel_multiplier=1).then_inc(consts, 1)

            pool.wait_ge(consts, NCONST - 1)
            nc.gpsimd.tensor_copy(region_bf[:], region_row[:]).then_inc(consts, 1)

            def x_root(g):
                pool.wait_ge(x_var_ready, g + 1)
                part = slice(g * XG, (g + 1) * XG)
                nc.gpsimd.tensor_tensor(x_rstd[:, part], x_var[:, part], minus_half[:, part],
                                        ALU.pow).then_inc(x_rstd_ready, 1)

            def fold(k, u, q, first=False):
                pool.wait_ge(a_loaded[u], 16 * (q + 1))
                if not first:
                    pool.wait_ge(row_step, 2 * k - 3 - u % 2)
                nc.gpsimd.tensor_tensor(folded[:, u % 2, :], a_rows[:, u, 0:HALF], a_rows[:, u, HALF:N],
                                        ALU.add).then_inc(fold_done, 1)

            def take_root(c):
                pool.wait_ge(row_step, 4 * c + 4)
                nc.gpsimd.tensor_tensor(root[:, bass.ds(2 * c, 2)], degree[:, bass.ds(2 * c, 2)],
                                        minus_half[:, 0:2], ALU.pow).then_inc(root_ready, 1)

            for g in range(NXG):
                x_root(g)
            fold(1, 1, 0, first=True)
            fold(2, 2, 0, first=True)
            take_root(0)
            fold(3, 3, 0)
            with pool.Fori(0, NT // RING - 1) as r:
                for u in range(0, RING, 2):
                    fold(RING * r + (RING + u), u, r + 1)
                    take_root(2 * r + (1 + u // 2))
                    fold(RING * r + (RING + u + 1), u + 1, r + 1)
            take_root(NPAIR - 1)

            pool.wait_ge(par_loaded, 16 * 4)
            whole = gate_b_row[:].unsqueeze(1).to_broadcast([1, 2, E])
            for n in range(3):
                rest = whole if n == 0 else gate_b_rest[:, n - 1]
                nc.gpsimd.tensor_copy(gate_b3[:, n], rest).then_inc(bias_step, 1)
                if n < 2:
                    pool.wait_ge(bias_step, 2 * n + 1)
                    nc.gpsimd.tensor_tensor(gate_b_rest[:, n], rest, gate_b3[:, n], ALU.subtract).then_inc(bias_step, 1)
                    pool.wait_ge(bias_step, 2 * n + 2)

            def group_root(g):
                n = GROUP[g][1]
                pool.wait_ge(var_ready, g + 1)
                nc.gpsimd.tensor_tensor(rstd[:, g % 2, 0:n], var[:, 0:n], minus_half[:, 0:n], ALU.pow).then_inc(rstd_ready, 1)

            def send_rows(g, lo, hi):
                pool.wait_ge(slot_ready, g + 1)
                pool.wait_ge(dest_ready, g + 1)
                u = g % RING
                for m in range(lo, hi):
                    t, k = m // TOPK, m % TOPK
                    nc.gpsimd.indirect_dma_start(
                        x_sorted, bass.IndirectOffsetOnAxis(ap=slot[:, u, k, t:t + 1], axis=0),
                        rows[:, u, t, k, :], None).then_inc(rows_sent[u], 16)

            group_root(0)
            group_root(1)
            for g in range(0, 2):
                send_rows(g, 0, 2)
                group_root(g + 2)
                send_rows(g, 2, 4)
            send_rows(2, 0, 4)
            pool_low = iter(POOL_LOW)
            for g in range(3, 6):
                send_rows(g, 0, 1)
                group_root(g + 1)
                send_rows(g, 1, 4)
                for e in islice(pool_low, (1, 2, 0)[g - 3]):
                    take_low(pool, nc.gpsimd.tensor_tensor, e, low_pool)
            group_root(7)
            send_rows(6, 0, 2)
            group_root(8)
            send_rows(6, 2, 4)
            send_rows(7, 0, 2)
            send_rows(8, 0, 2)
            for e in pool_low:
                take_low(pool, nc.gpsimd.tensor_tensor, e, low_pool)

            for t in range(NTILE):
                u = t % RING
                pool.wait_ge(y_ready, t + 1)
                nc.gpsimd.indirect_dma_start(
                    y_tokens, bass.IndirectOffsetOnAxis(ap=y_dest[:, u, :].bitcast(U32), axis=0),
                    y_out[:, u, :], None, bounds_check=SLOTS - 1, oob_is_err=False).then_inc(y_sent[u], 16)

        @block.tensor
        def _(pe):
            def keep_busy(n):
                for _ in range(n):
                    nc.tensor.matmul(bank[6][:, 0:P], ident[:], ident[:], start=True, stop=True)

            pe.wait_ge(consts, 3)
            keep_busy(10)
            pe.wait_ge(par_loaded, 16 * 4)
            nc.tensor.transpose(bank[4][:, 0:P], w_nat[:], ident[:])
            nc.tensor.matmul(bank[4][:, P:P + D], ones_row[:], b_row[:], start=True, stop=True).then_inc(wb_psum, 1)

            def support_transpose(g):
                pe.wait_ge(xn_ready, (g + 1) * XG)
                if g >= 2:
                    pe.wait_ge(xnt_ready, g - 1)
                for i in range(XG):
                    mm = nc.tensor.transpose(bank[5 + g % 2][:, i * P:(i + 1) * P], support[:, g * XG + i, :], ident[:])
                mm.then_inc(xnt_psum, 1)

            def support_product(g):
                pe.wait_ge(xnt_ready, g + 1)
                if g == 0:
                    pe.wait_ge(wb_ready, 2)
                else:
                    pe.wait_ge(sup_ready, g)
                for i in range(XG):
                    mm = nc.tensor.matmul(bank[7][:, i * D:(i + 1) * D], xn_t[:, g % 2, i * P:(i + 1) * P], w_t[:],
                                          start=True, stop=True)
                mm.then_inc(sup_psum, 1)

            blocks = adjT[:].rearrange("p (i j n) -> p i j n", i=NT, j=NT)

            def transpose_rows(k, u, q, first=False):
                pe.wait_ge(a_loaded[u], 16 * (q + 1))
                for g in range(GROUPS):
                    if not first:
                        pe.wait_ge(copied, (k - 1) * GROUPS + g + 1)
                    for j in range(BLOCKS):
                        at = (g * BLOCKS + j) * P
                        mm = nc.tensor.transpose(bank[g][:, j * P:(j + 1) * P], a_rows[:, u, at:at + P], ident[:])
                    mm.then_inc(transposed, 1)

            def eager(c, h, start=False, stop=False):
                pe.wait_ge(scale_step, 3 * c + 2)
                v = adjT[:, 0:EAGER * N].rearrange("p (i m) -> p i m", i=EAGER)
                for t in range(2):
                    mm = nc.tensor.matmul(bank[4][:], scaled_now[:, 2 * h + t, :],
                                          v[:, :, bass.ds(c * 2 * P + t * P, P)],
                                          start=start and t == 0, stop=stop and t == 1)
                if stop:
                    mm.then_inc(eager_done, 1)

            support_transpose(0)
            for k in range(RING):
                transpose_rows(k, k, 0, first=k == 0)
                if k + 1 < NXG:
                    support_transpose(k + 1)
                support_product(k)
            pe.wait_ge(copied, RING * GROUPS)
            eager(0, 0, start=True)
            with pe.Fori(0, NT // RING - 2) as r:
                for u in range(RING):
                    transpose_rows(RING * r + (RING + u), u, r + 1)
                    if u % 2:
                        h = u // 2
                        eager(2 * r + (1 + h), (1 + h) % 2)

            def gather(g, lo, hi):
                first, n = GROUP[g]
                if lo == 0 and g >= NEG + 2:
                    pe.wait_ge(mix_step, 3 * (g - 2) + 1)
                if g == NEG and hi >= NT:
                    pe.wait_ge(scale_step, 3 * NPAIR)
                for m in range(lo, hi):
                    t, j = m // NT, m % NT
                    mm = nc.tensor.matmul(acc_bank(g)[:, t * D:(t + 1) * D], blocks[:, first + t, j, :],
                                          scaled[:, j, :], start=j == 0, stop=j == NT - 1)
                if hi == n * NT:
                    mm.then_inc(acc_done, 1)

            def back(g):
                pe.wait_ge(acc_copied, g + 1)
                if g:
                    pe.wait_ge(mix_step, 3 * (g - 1) + 1)
                for t in range(2):
                    mm = nc.tensor.transpose(bank[2][:, t * P:(t + 1) * P], acc_sb[:, g % 2, t, :], ident[:])
                mm.then_inc(back_psum, 1)

            def turn_rows(g):
                pe.wait_ge(rows_ready, g + 1)
                if g:
                    pe.wait_ge(rowsT_ready, g)
                for t in range(GROUP[g][1]):
                    mm = nc.tensor.transpose(bank[3][:, t * P:(t + 1) * P], rows[:, g % RING, t, 0, 0:D], ident[:])
                mm.then_inc(rowsT_psum, 1)

            def logits(g):
                n = GROUP[g][1]
                if g:
                    pe.wait_ge(pick_step, 6 * (g - 1) + 2)
                else:
                    pe.wait_ge(bias_step, 5)
                for i in range(3):
                    nc.tensor.matmul(bank[5][:, 0:n * E], ones[0:1, :], gate_b3[:, i, 0:n, :], start=i == 0, stop=False)
                pe.wait_ge(rowsT_ready, g + 1)
                for t in range(n):
                    mm = nc.tensor.matmul(bank[5][:, t * E:(t + 1) * E], xT2[:, g % 2, t, :], gate_sb[:],
                                          start=False, stop=t == n - 1)
                mm.then_inc(logits_psum, 1)

            def ranks(g):
                n = GROUP[g][1]
                if g:
                    pe.wait_ge(gate_step, g)
                    pe.wait_ge(members_ready, g)
                o = bank[6][:, 0:n * E]
                nc.tensor.matmul(o, ones[0:1, :], region_bf[:, 0:n, :], start=True, stop=False)
                nc.tensor.matmul(o, ones[:], members[:, g % 2, :].unsqueeze(1).to_broadcast([P, n, E]),
                                 start=False, stop=False)
                pe.wait_ge(member_ready, g + 1)
                mm = nc.tensor.matmul(o, before[:], member[:, g % 2, 0:n, :], start=False, stop=n == 1)
                if n == 2:
                    mm = nc.tensor.matmul(bank[6][:, E:2 * E], ones[:], member[:, g % 2, 0, :], start=False, stop=True)
                mm.then_inc(rank_psum, 1)

            pe.wait_ge(consts, NCONST)
            q = NT // RING - 1
            transpose_rows(NT - 4, 0, q)
            transpose_rows(NT - 3, 1, q)
            eager(NPAIR - 3, 1)
            gather(2, 0, 2)
            transpose_rows(NT - 2, 2, q)
            gather(2, 2, 8)
            transpose_rows(NT - 1, 3, q)
            eager(NPAIR - 2, 0)
            pe.wait_ge(copied, NT * GROUPS)
            gather(2, 8, 12)
            pe.wait_ge(scale_step, 3 * (NPAIR - 1))
            gather(2, 12, NT - 2)
            eager(NPAIR - 1, 1, stop=True)
            gather(2, NT - 2, NT + 2)
            back(0)
            gather(2, 18, 24)
            back(1)
            gather(2, 24, 32)
            turn_rows(0)
            gather(3, 0, 4)
            logits(0)
            gather(3, 4, 13)
            ranks(0)
            gather(3, 13, 20)
            turn_rows(1)
            gather(3, 20, 23)
            logits(1)
            gather(3, 23, 32)
            gather(4, 0, 4)
            ranks(1)
            gather(4, 4, 5)
            turn_rows(2)
            gather(4, 5, 8)
            logits(2)
            gather(4, 8, 22)
            ranks(2)
            gather(4, 22, 24)
            turn_rows(3)
            gather(4, 24, 27)
            logits(3)
            gather(4, 27, 32)
            gather(5, 0, 5)
            ranks(3)
            gather(5, 5, 22)
            turn_rows(4)
            gather(5, 22, 25)
            logits(4)
            gather(5, 25, 32)
            gather(6, 0, 1)
            ranks(4)
            gather(6, 1, 18)
            turn_rows(5)
            gather(6, 18, 21)
            logits(5)
            gather(6, 21, 32)
            ranks(5)
            gather(7, 0, 16)
            turn_rows(6)
            gather(8, 0, 2)
            logits(6)
            gather(8, 2, 10)
            ranks(6)
            gather(8, 10, 16)
            turn_rows(7)
            logits(7)
            ranks(7)
            turn_rows(8)
            logits(8)
            ranks(8)

            pe.wait_ge(members_ready, NG)
            nc.tensor.matmul(bank[4][0:NTP, 0:E], ones[:, 0:NTP], members[:, NG % 2, :],
                             start=True, stop=True).then_inc(count_psum, 1)
            pe.wait_ge(tab_step, 9)
            for n in range(2):
                mm = nc.tensor.matmul(bank[7][0:1, n * NTP:(n + 1) * NTP], table_col[:, n:n + 1],
                                      ident[0:NTP, 0:NTP], start=True, stop=True)
            mm.then_inc(tab_psum, 1)

            keep_busy(8)

            pe.wait_ge(table_ready, 1)
            def step(s, u, q, stages, at):
                if 2 in stages:
                    v = (u - 3) % 2
                    pe.wait_ge(hid_ready, s - 2)
                    for c in range(HC):
                        mm = nc.tensor.transpose(bank[4 + v][:, c * P:(c + 1) * P], hid[:, v, c * P:(c + 1) * P],
                                                 ident[:])
                    mm.then_inc(hidT_psum, 1)
                if 3 in stages:
                    v = u % 2
                    pe.wait_ge(hidT_ready, s - 3)
                    if 2 not in stages:
                        pe.wait_ge(y_ready, s - 5)
                    for c in range(HC):
                        mm = nc.tensor.matmul(bank[6 + v][:, 0:D], hidT[:, v, c * P:(c + 1) * P],
                                              w_raw[:, bass.ds(at(4) + (W3 + c * D), D)], start=c == 0, stop=c == HC - 1)
                    mm.then_inc(y_psum, 1)
                if 0 in stages:
                    pe.wait_ge(xg_loaded[u], 16 * (q + 1))
                    nc.tensor.transpose(bank[u % 2][:, 0:P], xg[:, u, 0:D], ident[:]).then_inc(xgT_psum, 1)
                if 1 in stages:
                    v = (u - 1) % 2
                    if isinstance(s, int) and s == 1:
                        keep_busy(1)
                        for i in range(len(W_STAGE)):
                            pe.wait_ge(w_loaded[i], 16 * 4)
                        pe.wait_ge(low_dve, len(DVE_LOW))
                        pe.wait_ge(low_pool, len(POOL_LOW))
                    pe.wait_ge(xgT_ready, s)
                    low = w_parts[:, bass.ds(at(1) + LOW, BANK)]
                    high = w_parts[:, bass.ds(at(1) + HIGH, BANK)]
                    nc.tensor.matmul(bank[2 + v][:], xgT[:, 0, v, :], high, start=True, stop=False)
                    nc.tensor.matmul(bank[2 + v][:], xgT[:, 0, v, :], low, start=False, stop=False)
                    nc.tensor.matmul(bank[2 + v][:], xgT[:, 1, v, :], high, start=False, stop=True).then_inc(h_psum, 1)

            steps(pe, step, (0, 1, 3, 4), lambda first, n: load_values(pe, first + NTP, n, (E - 1) * WROW))

        @block.scalar
        def _(act):
            act.dma_start(w_nat[:], w_gnn).then_inc(par_loaded, 16)
            act.dma_start(b_row[:], b_gnn.rearrange("(a n) -> a n", a=1)).then_inc(par_loaded, 16)
            act.dma_start(gate_sb[:], gate_w).then_inc(par_loaded, 16)
            act.dma_start(gate_b_row[:], gate_b.rearrange("(a n) -> a n", a=1)).then_inc(par_loaded, 16)
            act.wait_ge(wb_psum, 1)
            nc.scalar.copy(w_t[:], bank[4][:, 0:P]).then_inc(wb_ready, 1)
            nc.scalar.copy(b_all[:], bank[4][:, P:P + D]).then_inc(wb_ready, 1)

            def copy_xn(g):
                act.wait_ge(xnt_psum, g + 1)
                if g >= 2:
                    act.wait_ge(sup_psum, g - 1)
                nc.scalar.copy(xn_t[:, g % 2, :], bank[5 + g % 2][:]).then_inc(xnt_ready, 1)

            def copy_rows(k):
                for g in range(GROUPS):
                    act.wait_ge(transposed, k * GROUPS + g + 1)
                    nc.scalar.copy(adjT[:, bass.ds(k * N + g * BANK, BANK)], bank[g][:]).then_inc(copied, 1)

            copy_xn(0)
            for k in range(RING):
                copy_rows(k)
                if k + 1 < NXG:
                    copy_xn(k + 1)
            with act.Fori(0, NT - RING) as k:
                copy_rows(RING + k)

            def copy_acc(g):
                act.wait_ge(eager_done, 1)
                nc.scalar.copy(acc_sb[:, g].rearrange("p t n -> p (t n)"),
                               bank[4][:, g * 2 * P:(g + 1) * 2 * P]).then_inc(acc_copied, 1)

            def route(g):
                first, n = GROUP[g]
                if g >= RING:
                    act.wait_ge(rows_sent[g % RING], sent(g - RING))
                nc.scalar.copy(rows[:, g % RING, 0:n, :, D + 1].bitcast(I32), dest[:, first:first + n, :]).then_inc(dest_ready, 1)
                act.wait_ge(rowsT_psum, g + 1)
                if g >= 2:
                    act.wait_ge(logits_psum, g - 1)
                nc.scalar.copy(xT2[:, g % 2, 0:n].rearrange("p t n -> p (t n)"), bank[3][:, 0:n * P]).then_inc(rowsT_ready, 1)
                act.wait_ge(gap_ready, g + 1)
                nc.scalar.activation(e_gap[:, 0:n], gap[:, 0:n], ACT.Exp).then_inc(e_ready, 1)

            act.wait_ge(consts, NCONST)
            for g in range(NEG):
                copy_acc(g)
            w_stage = iter(enumerate(W_STAGE))
            for g in range(NG):
                route(g)
                if g in (1, 2, 3, 4):
                    i, (lo, hi) = next(w_stage)
                    act.wait_ge(w_loaded[i], 16 * 4)
                    for e in range(lo, hi):
                        nc.scalar.copy(w_parts[:, e * WROW + HIGH:e * WROW + HIGH + BANK],
                                       w_raw[:, e * WROW + LOW:e * WROW + LOW + BANK]).then_inc(high_ready, 1)

            nc.scalar.activation(sil[:, 0, 0:1], minus_half[:, 0:1], ACT.Silu)

            def step(s, u, q, stages, at):
                if 0 in stages:
                    act.wait_ge(xgT_psum, s + 1)
                    nc.scalar.copy(xgT[:, 0, u % 2, :], bank[u % 2][:, 0:P]).then_inc(xgT_high, 1)
                if 1 in stages:
                    v = (u - 1) % 2
                    act.wait_ge(h_psum, s)
                    nc.scalar.activation(sil[:, v, :], bank[2 + v][:, 0:HID], ACT.Silu).then_inc(sil_ready, 1)
                if 2 in stages:
                    v = u % 2
                    act.wait_ge(hidT_psum, s - 1)
                    nc.scalar.copy(hidT[:, v, :], bank[4 + v][:, 0:HID]).then_inc(hidT_ready, 1)

            steps(act, step)

        @block.vector
        def _(dve):
            def x_moments(g):
                at = 2 * XG * g
                dve.wait_ge(x_loaded[g], 16)
                for n in range(XG):
                    nc.vector.bn_stats(x_stats[:, g * XG + n, :], x_mid[:, g * XG + n, :]).then_inc(x_stat, 1)
                for n in range(XG):
                    dve.wait_ge(x_stat, at + n + 1)
                    nc.vector.bn_aggr(x_mv[:, g * XG + n, :], x_stats[:, g * XG + n, :]).then_inc(x_stat, 1)
                dve.wait_ge(x_stat, at + 2 * XG)
                part = slice(g * XG, (g + 1) * XG)
                nc.vector.tensor_scalar(x_var[:, part], x_mv[:, part, 1], EPS, None, ALU.add).then_inc(x_var_ready, 1)

            def normalise_x(g):
                dve.wait_ge(x_rstd_ready, g + 1)
                for i in range(g * XG, (g + 1) * XG):
                    nc.vector.tensor_scalar(support[:, i, :], x_mid[:, i, :], x_mv[:, i, 0:1], x_rstd[:, i:i + 1],
                                            ALU.subtract, ALU.mult).then_inc(xn_ready, 1)

            def add_b(g):
                dve.wait_ge(sup_psum, g + 1)
                dve.wait_ge(wb_ready, 2)
                nc.vector.tensor_tensor(support[:, g * XG:(g + 1) * XG, :],
                                        bank[7][:].rearrange("p (i d) -> p i d", d=D),
                                        b_all[:].unsqueeze(1).to_broadcast([P, XG, D]), ALU.add).then_inc(sup_ready, 1)

            def sum_rows(k, u, first=False):
                if first:
                    dve.wait_ge(a_loaded[0], 16)
                else:
                    dve.wait_ge(fold_done, k)
                nc.vector.tensor_reduce(row_sum[:, bass.ds(k, 1)], a_rows[:, 0, :] if first else folded[:, u % 2, :],
                                        AX_X, ALU.add).then_inc(row_step, 1)

            def take_degree(c):
                pair = bass.ds(2 * c, 2)
                dve.wait_ge(row_step, 4 * c + 2)
                nc.vector.tensor_scalar(no_degree[:, pair], row_sum[:, pair], -1.0, None, ALU.is_equal).then_inc(row_step, 1)
                dve.wait_ge(row_step, 4 * c + 3)
                nc.vector.scalar_tensor_tensor(out=degree[:, pair], in0=row_sum[:, pair], scalar=1.0,
                                               in1=no_degree[:, pair], op0=ALU.add, op1=ALU.add).then_inc(row_step, 1)

            def scale_rows(c, h, first=False):
                pair = bass.ds(2 * c, 2)
                dve.wait_ge(root_ready, c + 1)
                nc.vector.tensor_tensor(dinv[:, pair], root[:, pair], no_degree[:, pair], ALU.subtract).then_inc(scale_step, 1)
                dve.wait_ge(scale_step, 3 * c + 1)
                if not first:
                    dve.wait_ge(transposed, 2 * c * GROUPS + 1)
                now = scaled_now[:, 2 * h:2 * h + 2, :]
                nc.vector.tensor_tensor(now, support[:, pair, :],
                                        dinv[:, pair].unsqueeze(2).to_broadcast([P, 2, D]), ALU.mult).then_inc(scale_step, 1)
                dve.wait_ge(scale_step, 3 * c + 2)
                nc.vector.tensor_copy(scaled[:, pair, :], now)
                for t in range(2):
                    row = x_mid[:, bass.ds(2 * c + t, 1), :].rearrange("p a d -> p (a d)")
                    v = nc.vector.scalar_tensor_tensor(out=row, in0=now[:, t, :], scalar=dinv[:, bass.ds(2 * c + t, 1)],
                                                       in1=row, op0=ALU.mult, op1=ALU.add)
                v.then_inc(scale_step, 1)

            x_moments(0)
            x_moments(1)
            normalise_x(0)
            x_moments(2)
            normalise_x(1)
            x_moments(3)
            sum_rows(0, 0, first=True)
            normalise_x(2)
            add_b(0)
            sum_rows(1, 1)
            take_degree(0)
            normalise_x(3)
            add_b(1)
            sum_rows(2, 2)
            scale_rows(0, 0, first=True)
            add_b(2)
            sum_rows(3, 3)
            take_degree(1)
            add_b(3)
            with dve.Fori(0, NT // RING - 1) as r:
                for h in range(2):
                    k, c = RING * r + (RING + 2 * h), 2 * r + (2 + h)
                    sum_rows(k, 0)
                    scale_rows(2 * r + (1 + h), (1 + h) % 2)
                    sum_rows(RING * r + (RING + 2 * h + 1), 1)
                    take_degree(c)
            scale_rows(NPAIR - 1, 1)

            def mix(g):
                first, n = GROUP[g]
                if g < NEG:
                    dve.wait_ge(back_psum, g + 1)
                    acc = bank[2]
                else:
                    dve.wait_ge(acc_done, g - NEG + 1)
                    acc = acc_bank(g)
                for t in range(n):
                    i = first + t
                    v = nc.vector.scalar_tensor_tensor(out=x_mid[:, i, :], in0=acc[:, t * D:(t + 1) * D],
                                                       scalar=dinv[:, i:i + 1], in1=x_mid[:, i, :],
                                                       op0=ALU.mult, op1=ALU.add)
                v.then_inc(mix_step, 1)
                dve.wait_ge(mix_step, 3 * g + 1)
                for t in range(n):
                    v = nc.vector.bn_stats(stats[:, t, :], x_mid[:, first + t, :])
                v.then_inc(mix_step, 1)
                dve.wait_ge(mix_step, 3 * g + 2)
                for t in range(n):
                    v = nc.vector.bn_aggr(mv[:, g % 2, t, :], stats[:, t, :])
                v.then_inc(mix_step, 1)
                dve.wait_ge(mix_step, 3 * g + 3)
                nc.vector.tensor_scalar(var[:, 0:n], mv[:, g % 2, 0:n, 1], EPS, None, ALU.add).then_inc(var_ready, 1)

            def fill_rows(g):
                first, n = GROUP[g]
                dve.wait_ge(rstd_ready, g + 1)
                if g >= RING:
                    dve.wait_ge(rows_sent[g % RING], sent(g - RING))
                for k in range(TOPK):
                    for t in range(n):
                        v = nc.vector.tensor_scalar(rows[:, g % RING, t, k, 0:D], x_mid[:, first + t, :],
                                                    mv[:, g % 2, t, 0:1], rstd[:, g % 2, t:t + 1],
                                                    ALU.subtract, ALU.mult)
                    if k == 0:
                        v.then_inc(rows_ready, 1)

            def choose(g):
                at = 6 * g
                n = GROUP[g][1]
                dve.wait_ge(logits_psum, g + 1)
                for t in range(n):
                    v = nc.vector.max(best[:, t, :], bank[5][:, t * E:(t + 1) * E])
                v.then_inc(pick_step, 1)
                dve.wait_ge(pick_step, at + 1)
                nc.vector.tensor_tensor(gap[:, 0:n], best[:, 0:n, 1], best[:, 0:n, 0], ALU.subtract).then_inc(gap_ready, 1)
                for t in range(n):
                    v = nc.vector.max_index(best_at[:, t, :], best[:, t, :], bank[5][:, t * E:(t + 1) * E])
                v.then_inc(pick_step, 1)
                dve.wait_ge(pick_step, at + 2)
                nc.vector.tensor_tensor(chosen[:, :, 0:n], iota_e[:].unsqueeze(1).unsqueeze(1).to_broadcast([P, TOPK, n, E]),
                                        best_at[:, 0:n, 0:TOPK].rearrange("p t k -> p k t").unsqueeze(3)
                                        .to_broadcast([P, TOPK, n, E]), ALU.is_equal).then_inc(pick_step, 1)
                dve.wait_ge(e_ready, g + 1)
                nc.vector.tensor_scalar(e_sum[:, 0:n], e_gap[:, 0:n], 1.0, None, ALU.add).then_inc(pick_step, 1)
                dve.wait_ge(pick_step, at + 3)
                nc.vector.tensor_tensor(member[:, g % 2, 0:n], chosen[:, 0, 0:n], chosen[:, 1, 0:n],
                                        ALU.add).then_inc(member_ready, 1)
                dve.wait_ge(pick_step, at + 4)
                nc.vector.reciprocal(rows[:, g % RING, 0:n, 0, D], e_sum[:, 0:n]).then_inc(pick_step, n % 2 + 1)
                dve.wait_ge(member_ready, g + 1)
                now, then = members[:, g % 2, :], members[:, (g + 1) % 2, :]
                if n == 2:
                    nc.vector.tensor_tensor(members[:, 2, :], now, member[:, g % 2, 0, :], ALU.add).then_inc(pick_step, 1)
                else:
                    nc.vector.tensor_tensor(then, now, member[:, g % 2, 0, :], ALU.add).then_inc(members_ready, 1)
                dve.wait_ge(pick_step, at + 5)
                nc.vector.tensor_tensor(rows[:, g % RING, 0:n, 1, D], e_gap[:, 0:n], rows[:, g % RING, 0:n, 0, D], ALU.mult)
                if n == 2:
                    dve.wait_ge(pick_step, at + 6)
                    nc.vector.tensor_tensor(then, members[:, 2, :], member[:, g % 2, 1, :], ALU.add).then_inc(members_ready, 1)

            def place(g):
                n = GROUP[g][1]
                dve.wait_ge(rank_psum, g + 1)
                nc.vector.tensor_tensor(picked[:, :, 0:n], chosen[:, :, 0:n],
                                        bank[6][:, 0:n * E].rearrange("p (t e) -> p t e", t=n).unsqueeze(1)
                                        .to_broadcast([P, TOPK, n, E]), ALU.mult).then_inc(gate_step, 1)
                dve.wait_ge(gate_step, g + 1)
                with nc.allow_low_precision(reason="one term is not zero, a whole number below 2^24"):
                    nc.vector.tensor_reduce(slot[:, g % RING, :, 0:n], picked[:, :, 0:n], AX_X, ALU.add).then_inc(slot_ready, 1)

            dve.wait_ge(consts, NCONST)
            dve.wait_ge(scale_step, 3 * NPAIR)
            dve_low = iter(DVE_LOW)

            def low_parts(n):
                for e in islice(dve_low, n):
                    take_low(dve, nc.vector.tensor_tensor, e, low_dve)

            mix(0)
            fill_rows(0)
            for g in range(1, 4):
                mix(g)
                choose(g - 1)
                fill_rows(g)
                place(g - 1)
            choose(3)
            place(3)
            for g in range(4, NG - 3):
                mix(g)
                low_parts(1)
                fill_rows(g)
                low_parts(1)
                choose(g)
                place(g)
            mix(NG - 3)
            low_parts(1)
            fill_rows(NG - 3)
            for g in range(NG - 2, NG):
                mix(g)
                choose(g - 1)
                if g == NG - 1:
                    fill_rows(g)
                place(g - 1)
                if g == NG - 2:
                    fill_rows(g)
            choose(NG - 1)
            place(NG - 1)

            chain = [0]

            def link(*ops):
                chain[0] += 1
                ops[-1].then_inc(tab_step, 1)
                dve.wait_ge(tab_step, chain[0])

            dve.wait_ge(count_psum, 1)
            count = bank[4][0:NTP, 0:E]
            v = nc.vector.tensor_scalar(cnt_up[:], count, float(P - 1), None, ALU.add)
            link(v, nc.vector.tensor_tensor(end_row[:], count, region_col[:], ALU.add))
            link(nc.vector.tensor_scalar(tiles_i[:], cnt_up[:], P.bit_length() - 1, None, ALU.arith_shift_right))
            link(nc.vector.tensor_copy(tiles_f[:], tiles_i[:]))
            link(nc.vector.tensor_tensor_scan(upto[:], tiles_f[:], zeros_e[:], 0.0, ALU.add, ALU.add))
            v = nc.vector.tensor_tensor(prior[:], upto[:], tiles_f[:], ALU.subtract)
            link(v, nc.vector.tensor_scalar(passed[:], upto[:], tile_no[:], 0.0, ALU.is_le, ALU.add, accum_out=n_passed[:]))
            v = nc.vector.scalar_tensor_tensor(out=first_row[:], in0=prior[:], scalar=float(P), in1=end_row[:],
                                               op0=ALU.mult, op1=ALU.add)
            v = nc.vector.scalar_tensor_tensor(out=is_own[:], in0=prior[:], scalar=tile_no[:], in1=passed[:],
                                               op0=ALU.is_le, op1=ALU.subtract)
            v = nc.vector.tensor_scalar(live[:], n_passed[:], float(E), None, ALU.is_lt)
            link(v, nc.vector.tensor_scalar(table_col[:, 1:2], n_passed[:], float(E - 1), float(WROW), ALU.min, ALU.mult))
            link(nc.vector.scalar_tensor_tensor(out=picked_row[:], in0=is_own[:], scalar=1.0, in1=first_row[:],
                                                op0=ALU.mult, op1=ALU.mult, accum_out=start_sum[:]))
            link(nc.vector.tensor_scalar(start_row[:], start_sum[:], tile_row[:], float(-NULL_ROW), ALU.subtract, ALU.add))
            nc.vector.tensor_scalar(table_col[:, 0:1], start_row[:], live[:], float(NULL_ROW), ALU.mult,
                                    ALU.add).then_inc(tab_step, 1)
            dve.wait_ge(tab_psum, 1)
            nc.vector.tensor_copy(table[:], bank[7][0:1, 0:2 * NTP]).then_inc(table_ready, 1)
            low_parts(len(DVE_LOW))

            def step(s, u, q, stages, at):
                if 0 in stages:
                    dve.wait_ge(xgT_high, s + 1)
                    nc.vector.tensor_tensor(xgT[:, 1, u % 2, :], bank[u % 2][:, 0:P],
                                            xgT[:, 0, u % 2, :].bitcast(F32), ALU.subtract).then_inc(xgT_ready, 1)
                    if not isinstance(s, int) or s >= RING:
                        dve.wait_ge(y_ready, s - LAG)
                    nc.vector.tensor_copy(meta[:, u, :], xg[:, u, D:ROW]).then_inc(meta_ready, 1)
                if 1 in stages:
                    v = (u - 1) % 2
                    dve.wait_ge(sil_ready, s)
                    nc.vector.tensor_tensor(hid[:, v, :], sil[:, v, :], bank[2 + v][:, HID:BANK],
                                            ALU.mult).then_inc(hid_ready, 1)
                if 3 in stages:
                    v, w = (u - 3) % 2, (u - 3) % RING
                    dve.wait_ge(y_psum, s - 2)
                    if not isinstance(s, int) or s - LAG >= RING:
                        dve.wait_ge(y_sent[w], 16 * (q_of(s, q, u)))
                    dve.wait_ge(meta_ready, s - 2)
                    nc.vector.tensor_copy(y_dest[:, w, :], meta[:, w, 1:2])
                    nc.vector.tensor_scalar(y_out[:, w, :], bank[6 + v][:, 0:D], meta[:, w, 0:1], None,
                                            ALU.mult).then_inc(y_ready, 1)

            def q_of(s, q, u):
                return q - (1 if u < LAG else 0)

            steps(dve, step)

            for q, part in enumerate(PART):
                dve.wait_ge(z_loaded[q], 16)
                nc.vector.tensor_tensor(z_buf[:, part, 0, :], z_buf[:, part, 0, :], z_buf[:, part, 1, :],
                                        ALU.add).then_inc(z_sum, 1)
                dve.wait_ge(z_sum, q + 1)
                nc.vector.tensor_tensor(x_mid[:, part, :], x_mid[:, part, :], z_buf[:, part, 0, :],
                                        ALU.add).then_inc(out_ready, 1)


_INS = ["x", "adj", "L0_gnn_W", "L0_gnn_b", "L0_ffn_gate_w", "L0_ffn_gate_b", "L0_ffn_w1", "L0_ffn_w2", "L0_ffn_w3"]


def kernel(**inputs):
    import concourse.bacc as bacc
    from concourse.bass_utils import run_bass_kernel_spmd

    nc = bacc.Bacc("TRN2", target_bir_lowering=False, num_devices=1)
    arrays, args = {}, []
    for name in _INS:
        a = np.ascontiguousarray(inputs[name])
        arrays[f"in_{name}"] = a
        args.append(nc.dram_tensor(f"in_{name}", a.shape, mybir.dt.from_np(a.dtype), kind="ExternalInput").ap())
    out = nc.dram_tensor("out", inputs["x"].shape, F32, kind="ExternalOutput").ap()
    graph_moe(nc, *args, out)
    r = run_bass_kernel_spmd(nc, [arrays], core_ids=[0])
    return r.results[0]["out"]
```
